# Optimizing a Trainium2 kernel written in Bass

```python
import numpy as np
import jax
import jax.numpy as jnp

def _softmax(x, axis=-1):
    return jax.nn.softmax(x, axis=axis)

def _gelu(x):
    return jax.nn.gelu(x, approximate=True)

def _silu(x):
    return jax.nn.silu(x)

def _sigmoid(x):
    return jax.nn.sigmoid(x)

def _layernorm(x, axis=-1, eps=1e-05):
    m = jnp.mean(x, axis=axis, keepdims=True)
    v = jnp.var(x, axis=axis, keepdims=True)
    return (x - m) / jnp.sqrt(v + eps)

def _scatter_add(tgt, idx, src, axis=0):
    return tgt.at[idx].add(src)

def _segment_sum(src, seg, n):
    return jax.ops.segment_sum(src, seg, n)
kernel_name = 'mk_flamingo_gated_d2_seqx_r8_311dfb'

def setup_inputs(seed: int=0):
    np.random.seed(seed)
    _w = jnp.asarray

    def _rec_inputs():
        import jax
        import jax.numpy as jnp
        _rk = jax.random.key(seed)
        x = 7.22e-05 + 1 * jax.random.normal(jax.random.fold_in(_rk, 1), (4, 512, 128), jnp.float32)
        _lenS = 512 - jax.random.randint(jax.random.fold_in(_rk, 7), (4,), 0, max(1, 512 // 4) + 1, jnp.int32)
        _lenS2 = 32 - jax.random.randint(jax.random.fold_in(_rk, 8), (4,), 0, max(1, 32 // 4) + 1, jnp.int32)
        _ctx_768P = jax.random.normal(jax.random.fold_in(_rk, 11), (4, 16, 96), jnp.float32)
        _ctx_768c = jax.random.dirichlet(jax.random.fold_in(_rk, 511), 0.3 * jnp.ones((16,), jnp.float32), (4, 32))
        _ctx_768t = jnp.einsum('bsk,bkd->bsd', _ctx_768c, _ctx_768P)
        _ctx_768t = _ctx_768t * jax.lax.rsqrt(jnp.mean(jnp.square(_ctx_768t)) + 1e-12) * 0.953939
        ctx_768 = 2.09791e-05 + 1.00001 * (_ctx_768t + 0.3 * jax.random.normal(jax.random.fold_in(_rk, 611), (4, 32, 96), jnp.float32))
        _validS = jnp.arange(512)[None, :] < _lenS[:, None]
        _validS2 = jnp.arange(32)[None, :] < _lenS2[:, None]
        _causal = jnp.tril(jnp.ones((512, 512), dtype=bool))
        mask_BxS2_bf1 = jnp.ones((4, 32), dtype=bool)
        _g = jax.random.normal(jax.random.fold_in(_rk, 9001), (2, 2), jnp.float32)
        _g = jnp.sign(_g) * jnp.maximum(jnp.abs(_g), 1.0) + (_g == 0) * 1.0
        g_xattn = _g[0]
        g_ffn = _g[1]
        return (x, ctx_768, mask_BxS2_bf1, g_xattn, g_ffn)
    x, ctx_768, mask_BxS2_bf1, g_xattn, g_ffn = _rec_inputs()

    def _L0_xattn_setup():
        import jax, jax.numpy as jnp
        import numpy as np
        HEADS = 8
        DIM_HEAD = 64
        SCALE = DIM_HEAD ** (-0.5)
        key = jax.random.key(seed)
        ks = jax.random.split(key, 7)
        b, n, m = (4, 256, 128)
        qd, cd, inner = (128, 96, HEADS * DIM_HEAD)
        s = lambda fan_in: 1.0 / np.sqrt(fan_in)
        return {'x': jax.random.normal(ks[0], (b, n, qd), jnp.float32), 'context': jax.random.normal(ks[1], (b, m, cd), jnp.float32), 'Wq': jax.random.normal(ks[2], (qd, inner), jnp.float32) * s(qd), 'Wk': jax.random.normal(ks[3], (cd, inner), jnp.float32) * s(cd), 'Wv': jax.random.normal(ks[4], (cd, inner), jnp.float32) * s(cd), 'Wout': jax.random.normal(ks[5], (inner, qd), jnp.float32) * s(inner), 'bout': jax.random.normal(ks[6], (qd,), jnp.float32) * 0.01}
    _L0_xattn_all = _L0_xattn_setup()
    _L0_xattn_in = {k: v for k, v in _L0_xattn_all.items() if k in ('Wq', 'Wk', 'Wv', 'Wout', 'bout')}
    del _L0_xattn_all

    def _L0_ffn_setup():
        import jax, jax.numpy as jnp
        import numpy as np
        B, T, D = (1, 256, 128)
        E, DFF = (8, 512)

        def _gating(logits):
            S, num_e = logits.shape
            gates = jax.nn.softmax(logits.astype(jnp.float32), axis=1)
            idx1 = jnp.argmax(gates, axis=1)
            mask1 = jax.nn.one_hot(idx1, num_e, dtype=jnp.int32)
            logits_ex1 = jnp.where(mask1.astype(bool), -jnp.inf, logits)
            idx2 = jnp.argmax(logits_ex1, axis=1)
            mask2 = jax.nn.one_hot(idx2, num_e, dtype=jnp.int32)
            loc1 = jnp.cumsum(mask1, axis=0) - 1
            loc2 = jnp.cumsum(mask2, axis=0) - 1 + jnp.sum(mask1, axis=0, keepdims=True)
            loc1_s = jnp.sum(loc1 * mask1, axis=1)
            loc2_s = jnp.sum(loc2 * mask2, axis=1)
            g1 = jnp.sum(gates * mask1, axis=1)
            g2 = jnp.sum(gates * mask2, axis=1)
            denom = jnp.maximum(g1 + g2, jnp.finfo(jnp.float32).eps)
            g1, g2 = (g1 / denom, g2 / denom)
            cap = S
            loc1_sc = jax.nn.one_hot(loc1_s, cap, dtype=jnp.float32)
            loc2_sc = jax.nn.one_hot(loc2_s, cap, dtype=jnp.float32)
            combine = (g1[:, None] * mask1)[:, :, None] * loc1_sc[:, None, :] + (g2[:, None] * mask2)[:, :, None] * loc2_sc[:, None, :]
            dispatch_mask = combine != 0
            return (combine.astype(logits.dtype), dispatch_mask)
        key = jax.random.key(seed)
        k1, k2, k3, k4 = jax.random.split(key, 4)
        x = jax.random.normal(k1, (B, T, D), dtype=jnp.float32)
        Wg = jax.random.normal(k2, (D, E), dtype=jnp.float32) * (1.0 / np.sqrt(D))
        w1 = jax.random.normal(k3, (D, DFF), dtype=jnp.float32) * (1.0 / np.sqrt(D))
        w2 = jax.random.normal(k4, (DFF, D), dtype=jnp.float32) * (1.0 / np.sqrt(DFF))
        return {'x': x, 'Wg': Wg, 'w1': w1, 'w2': w2}
    _L0_ffn_all = _L0_ffn_setup()
    _L0_ffn_in = {k: v for k, v in _L0_ffn_all.items() if k in ('Wg', 'w1', 'w2')}
    del _L0_ffn_all

    def _L1_xattn_setup():
        import jax, jax.numpy as jnp
        import numpy as np
        DIM = 128
        CTX_DIM = 96
        HEADS = 16
        key = jax.random.key(seed)
        ks = jax.random.split(key, 7)
        B, N, M = (4, 512, 32)
        x = jax.random.normal(ks[0], (B, N, DIM), dtype=jnp.float32)
        context = jax.random.normal(ks[1], (B, M, CTX_DIM), dtype=jnp.float32)
        context_mask = jnp.ones((B, M), dtype=bool)
        s_d = 1.0 / np.sqrt(DIM)
        s_c = 1.0 / np.sqrt(CTX_DIM)
        Wq = jax.random.normal(ks[2], (DIM, DIM), dtype=jnp.float32) * s_d
        Wk = jax.random.normal(ks[3], (CTX_DIM, DIM), dtype=jnp.float32) * s_c
        Wv = jax.random.normal(ks[4], (CTX_DIM, DIM), dtype=jnp.float32) * s_c
        Wo = jax.random.normal(ks[5], (DIM, DIM), dtype=jnp.float32) * s_d
        return {'x': x, 'context': context, 'context_mask': context_mask, 'Wq': Wq, 'Wk': Wk, 'Wv': Wv, 'Wo': Wo}
    _L1_xattn_all = _L1_xattn_setup()
    _L1_xattn_in = {k: v for k, v in _L1_xattn_all.items() if k in ('Wq', 'Wk', 'Wv', 'Wo')}
    del _L1_xattn_all

    def _L1_ffn_setup():
        import jax, jax.numpy as jnp
        import numpy as np
        E, K = (8, 4)
        B, S, D = (4, 128, 128)
        H = D * 2 * 4 // 3

        def _swiglu(u, w1, w2, w3):
            h = jnp.einsum('...d,hd->...h', u, w1)
            v = jnp.einsum('...d,hd->...h', u, w2)
            return jnp.einsum('...h,dh->...d', jax.nn.sigmoid(h) * h * v, w3)
        key = jax.random.key(seed)
        ks = jax.random.split(key, 9)
        std = 0.02
        return {'x': jax.random.normal(ks[0], (B, S, D), jnp.float32), 'Wg': jax.random.normal(ks[1], (E, D), jnp.float32) * std, 'routing_bias': jnp.zeros((E,), jnp.float32), 'W1': jax.random.normal(ks[2], (E, H, D), jnp.float32) * std, 'W2': jax.random.normal(ks[3], (E, H, D), jnp.float32) * std, 'W3': jax.random.normal(ks[4], (E, D, H), jnp.float32) * std, 'Ws1': jax.random.normal(ks[5], (H, D), jnp.float32) * std, 'Ws2': jax.random.normal(ks[6], (H, D), jnp.float32) * std, 'Ws3': jax.random.normal(ks[7], (D, H), jnp.float32) * std}
    _L1_ffn_all = _L1_ffn_setup()
    _L1_ffn_in = {k: v for k, v in _L1_ffn_all.items() if k in ('Wg', 'routing_bias', 'W1', 'W2', 'W3', 'Ws1', 'Ws2', 'Ws3')}
    del _L1_ffn_all
    return {'x': x, 'ctx_768': ctx_768, 'mask_BxS2_bf1': mask_BxS2_bf1, 'g_xattn': g_xattn, 'g_ffn': g_ffn, 'L0_xattn_Wq': _L0_xattn_in['Wq'], 'L0_xattn_Wk': _L0_xattn_in['Wk'], 'L0_xattn_Wv': _L0_xattn_in['Wv'], 'L0_xattn_Wout': _L0_xattn_in['Wout'], 'L0_xattn_bout': _L0_xattn_in['bout'], 'L0_ffn_Wg': _L0_ffn_in['Wg'], 'L0_ffn_w1': _L0_ffn_in['w1'], 'L0_ffn_w2': _L0_ffn_in['w2'], 'L1_xattn_Wq': _L1_xattn_in['Wq'], 'L1_xattn_Wk': _L1_xattn_in['Wk'], 'L1_xattn_Wv': _L1_xattn_in['Wv'], 'L1_xattn_Wo': _L1_xattn_in['Wo'], 'L1_ffn_Wg': _L1_ffn_in['Wg'], 'L1_ffn_routing_bias': _L1_ffn_in['routing_bias'], 'L1_ffn_W1': _L1_ffn_in['W1'], 'L1_ffn_W2': _L1_ffn_in['W2'], 'L1_ffn_W3': _L1_ffn_in['W3'], 'L1_ffn_Ws1': _L1_ffn_in['Ws1'], 'L1_ffn_Ws2': _L1_ffn_in['Ws2'], 'L1_ffn_Ws3': _L1_ffn_in['Ws3']}

def reference(x, ctx_768, mask_BxS2_bf1, g_xattn, g_ffn, L0_xattn_Wq, L0_xattn_Wk, L0_xattn_Wv, L0_xattn_Wout, L0_xattn_bout, L0_ffn_Wg, L0_ffn_w1, L0_ffn_w2, L1_xattn_Wq, L1_xattn_Wk, L1_xattn_Wv, L1_xattn_Wo, L1_ffn_Wg, L1_ffn_routing_bias, L1_ffn_W1, L1_ffn_W2, L1_ffn_W3, L1_ffn_Ws1, L1_ffn_Ws2, L1_ffn_Ws3):
    import jax
    import jax.numpy as jnp

    def _L0_xattn_ref(x, context, Wq, Wk, Wv, Wout, bout):
        import jax, jax.numpy as jnp
        import numpy as np
        HEADS = 8
        DIM_HEAD = 64
        SCALE = DIM_HEAD ** (-0.5)
        b, n, _ = x.shape
        m = context.shape[1]
        q = (x @ Wq).reshape(b, n, HEADS, DIM_HEAD)
        k = (context @ Wk).reshape(b, m, HEADS, DIM_HEAD)
        v = (context @ Wv).reshape(b, m, HEADS, DIM_HEAD)
        sim = jnp.einsum('bihd,bjhd->bhij', q, k) * SCALE
        attn = jax.nn.softmax(sim, axis=-1)
        out = jnp.einsum('bhij,bjhd->bihd', attn, v).reshape(b, n, HEADS * DIM_HEAD)
        return out @ Wout + bout

    def _L0_ffn_ref(x, Wg, w1, w2):
        import jax, jax.numpy as jnp
        import numpy as np
        B, T, D = (1, 256, 128)
        E, DFF = (8, 512)

        def _gating(logits):
            S, num_e = logits.shape
            gates = jax.nn.softmax(logits.astype(jnp.float32), axis=1)
            idx1 = jnp.argmax(gates, axis=1)
            mask1 = jax.nn.one_hot(idx1, num_e, dtype=jnp.int32)
            logits_ex1 = jnp.where(mask1.astype(bool), -jnp.inf, logits)
            idx2 = jnp.argmax(logits_ex1, axis=1)
            mask2 = jax.nn.one_hot(idx2, num_e, dtype=jnp.int32)
            loc1 = jnp.cumsum(mask1, axis=0) - 1
            loc2 = jnp.cumsum(mask2, axis=0) - 1 + jnp.sum(mask1, axis=0, keepdims=True)
            loc1_s = jnp.sum(loc1 * mask1, axis=1)
            loc2_s = jnp.sum(loc2 * mask2, axis=1)
            g1 = jnp.sum(gates * mask1, axis=1)
            g2 = jnp.sum(gates * mask2, axis=1)
            denom = jnp.maximum(g1 + g2, jnp.finfo(jnp.float32).eps)
            g1, g2 = (g1 / denom, g2 / denom)
            cap = S
            loc1_sc = jax.nn.one_hot(loc1_s, cap, dtype=jnp.float32)
            loc2_sc = jax.nn.one_hot(loc2_s, cap, dtype=jnp.float32)
            combine = (g1[:, None] * mask1)[:, :, None] * loc1_sc[:, None, :] + (g2[:, None] * mask2)[:, :, None] * loc2_sc[:, None, :]
            dispatch_mask = combine != 0
            return (combine.astype(logits.dtype), dispatch_mask)
        d_model = x.shape[2]
        xs = x.reshape(-1, d_model)
        logits = xs @ Wg
        combine, dispatch_mask = _gating(logits)
        dispatched = jnp.einsum('sec,sm->ecm', dispatch_mask.astype(jnp.float32), xs)
        expert_out = jax.nn.relu(dispatched @ w1) @ w2
        out = jnp.einsum('sec,ecm->sm', combine, expert_out)
        return out.reshape(x.shape)

    def _L1_xattn_ref(x, context, context_mask, Wq, Wk, Wv, Wo):
        import jax, jax.numpy as jnp
        import numpy as np
        DIM = 128
        CTX_DIM = 96
        HEADS = 16
        B, N, _ = x.shape
        M = context.shape[1]
        hd = DIM // HEADS
        scale = hd ** (-0.5)
        q = (x @ Wq).reshape(B, N, HEADS, hd).transpose(0, 2, 1, 3)
        k = (context @ Wk).reshape(B, M, HEADS, hd).transpose(0, 2, 1, 3)
        v = (context @ Wv).reshape(B, M, HEADS, hd).transpose(0, 2, 1, 3)
        scores = jnp.einsum('bhid,bhjd->bhij', q, k) * scale
        max_neg = -jnp.finfo(scores.dtype).max
        scores = jnp.where(context_mask[:, None, None, :], scores, max_neg)
        attn = jax.nn.softmax(scores, axis=-1)
        out = jnp.einsum('bhij,bhjd->bhid', attn, v)
        out = out.transpose(0, 2, 1, 3).reshape(B, N, DIM)
        return out @ Wo

    def _L1_ffn_ref(x, Wg, routing_bias, W1, W2, W3, Ws1, Ws2, Ws3):
        import jax, jax.numpy as jnp
        import numpy as np
        E, K = (8, 4)
        B, S, D = (4, 128, 128)
        H = D * 2 * 4 // 3

        def _swiglu(u, w1, w2, w3):
            h = jnp.einsum('...d,hd->...h', u, w1)
            v = jnp.einsum('...d,hd->...h', u, w2)
            return jnp.einsum('...h,dh->...d', jax.nn.sigmoid(h) * h * v, w3)
        gate = jnp.einsum('bsd,ed->bse', x, Wg) + routing_bias
        _, top_idx = jax.lax.top_k(gate, K)
        mask = jax.nn.one_hot(top_idx, E, dtype=gate.dtype).sum(-2)
        masked_gate = jnp.where(mask > 0, gate, -jnp.inf)
        probs = jax.nn.softmax(masked_gate, axis=-1)
        weights = probs * mask
        out = _swiglu(x, Ws1, Ws2, Ws3)
        h1 = jnp.einsum('bsd,ehd->ebsh', x, W1)
        h2 = jnp.einsum('bsd,ehd->ebsh', x, W2)
        eo = jnp.einsum('ebsh,edh->ebsd', jax.nn.sigmoid(h1) * h1 * h2, W3)
        out = out + jnp.einsum('ebsd,bse->bsd', eo, weights)
        return out
    x = x + jnp.tanh(g_xattn[0]) * _L0_xattn_ref(_layernorm(x, axis=-1), ctx_768, L0_xattn_Wq, L0_xattn_Wk, L0_xattn_Wv, L0_xattn_Wout, L0_xattn_bout)
    x = x + jnp.tanh(g_ffn[0]) * _L0_ffn_ref(_layernorm(x, axis=-1), L0_ffn_Wg, L0_ffn_w1, L0_ffn_w2)
    x = x + jnp.tanh(g_xattn[1]) * _L1_xattn_ref(_layernorm(x, axis=-1), ctx_768, mask_BxS2_bf1, L1_xattn_Wq, L1_xattn_Wk, L1_xattn_Wv, L1_xattn_Wo)
    x = x + jnp.tanh(g_ffn[1]) * _L1_ffn_ref(_layernorm(x, axis=-1), L1_ffn_Wg, L1_ffn_routing_bias, L1_ffn_W1, L1_ffn_W2, L1_ffn_W3, L1_ffn_Ws1, L1_ffn_Ws2, L1_ffn_Ws3)
    return x

_drawn_inputs = setup_inputs


def setup_inputs(seed=0):
    import zlib

    import numpy as np

    out = dict(_drawn_inputs(seed))
    spreads = {'g_ffn': (-1.0, 0.6), 'L1_ffn_routing_bias': (0.0, 0.8)}
    factors = {'L0_xattn_bout': 7.86,
     'L0_ffn_Wg': 8.0,
     'L1_ffn_Wg': 8.0,
     'L1_ffn_W1': 8.0,
     'L1_ffn_W2': 8.0,
     'L1_ffn_W3': 8.0,
     'L1_ffn_Ws1': 8.0,
     'L1_ffn_Ws2': 8.0,
     'L1_ffn_Ws3': 8.0}
    for name, (base, spread) in spreads.items():
        noise = np.random.default_rng([zlib.crc32(name.encode()), seed]).standard_normal(out[name].shape)
        drawn = base * np.exp(spread * noise) if base else spread * noise
        out[name] = jnp.asarray(drawn.astype(out[name].dtype))
    for name, factor in factors.items():
        out[name] = (out[name] * factor).astype(out[name].dtype)
    return out
```

```python
import concourse.bass as bass
from concourse import mybir
from contextlib import ExitStack

ROWS, D = 128, 128
UNITS, TILES = 4, 16
PER_UNIT = TILES // UNITS
UTOK = ROWS * PER_UNIT
KEYS, CTX = 32, 96
HEADS = (8, 16)
HEAD_DIM = (64, 8)
DFF0 = 512
CH0 = DFF0 // ROWS
EXPERTS = 8
HID = D * 2 * 4 // 3
CHUNKS = (ROWS, ROWS, HID - 2 * ROWS)
NCH = len(CHUNKS)
ECOLS = 2 * HID + NCH * D
FF0COLS = DFF0 + CH0 * D + 2 * EXPERTS
EPS = 1e-5
F32_EPS = 1.1920928955078125e-07
LOWEST_BF16 = -3.3895313892515355e38


def flamingo_kernel(nc, x, ctx_t, mask, gx, gf, wk0, wq0t, wv0, wo0, bout, wk1, wq1t, wv1, wo1,
                    head_mask, ff0, ew, bias1, ident_in, gate_scratch, out):
    f32, f32r, bf16 = mybir.dt.float32, mybir.dt.float32r, mybir.dt.bfloat16
    ALU, ACT, AX = mybir.AluOpType, mybir.ActivationFunctionType, mybir.AxisListType

    ctx = ExitStack()
    with ctx:
        def sb(name, shape, dt=f32):
            return ctx.enter_context(nc.sbuf_tensor(name, shape, dt))

        def sem(name):
            return ctx.enter_context(nc.semaphore(name))

        X = sb("X", [ROWS, TILES, D])
        ident = sb("ident", [ROWS, D])
        ew_raw = sb("ew_raw", [ROWS, 2, ECOLS])
        ewh = sb("ewh", [ROWS, 1 + EXPERTS, ECOLS], f32r)
        ewl = sb("ewl", [ROWS, 1 + EXPERTS, ECOLS], f32r)
        ff0h = sb("ff0h", [ROWS, FF0COLS], f32r)
        ff0l = sb("ff0l", [ROWS, FF0COLS], f32r)
        GH = [sb(f"g{i}_hi", [ROWS, UNITS, HEADS[i] * KEYS], f32r) for i in range(2)]
        GL = [sb(f"g{i}_lo", [ROWS, UNITS, HEADS[i] * KEYS], f32r) for i in range(2)]
        VW = [sb(f"vw{i}", [ROWS, UNITS * HEADS[i] // 4, D]) for i in range(2)]
        xth = sb("xt_hi", [ROWS, UNITS * UTOK], f32r)
        xtl = sb("xt_lo", [ROWS, UNITS * UTOK], f32r)
        acth = sb("act_hi", [ROWS, 3, UTOK], f32r)
        actl = sb("act_lo", [ROWS, 3, UTOK], f32r)
        xn = sb("xn", [ROWS, 2, PER_UNIT, D])
        oT = sb("oT", [ROWS, UTOK])
        wT = sb("wT", [EXPERTS, UTOK])
        arena = sb("arena", [ROWS, 14 * UTOK])
        SC = [arena[:, UTOK * i:UTOK * (i + 1)] for i in range(6)]
        PTS = arena[:, 6 * UTOK:14 * UTOK].rearrange("p (i c n) -> p i c n", i=2, c=4)
        wk0_sb, wv0_sb = SC[4], SC[5]
        big = arena[:, 6 * UTOK:14 * UTOK].rearrange("p (i h n) -> p i h n", i=4, h=8)
        wq0_sb, wo0_sb, kT0, vT0 = (big[0:64, i] for i in range(4))
        KB = PTS[:, 0]
        VB = PTS[:, 1]
        silu = arena[:, 0:3 * UTOK].rearrange("p (i n) -> p i n", i=3)
        act = arena[:, 3 * UTOK:6 * UTOK].rearrange("p (i n) -> p i n", i=3)
        acc = arena[:, 6 * UTOK:7 * UTOK]
        gated = arena[:, 8 * UTOK:10 * UTOK].rearrange("p (i n) -> p i n", i=2)
        wb = arena[:, 10 * UTOK:14 * UTOK].rearrange("p (i n) -> p i n", i=4)
        ctx_sb = sb("ctx_sb", [CTX, ROWS])
        wk1_sb, wv1_sb = sb("wk1_sb", [CTX, D]), sb("wv1_sb", [CTX, D])
        wq1_sb, wo1_sb = sb("wq1_sb", [D, D]), sb("wo1_sb", [D, D])
        kv1 = sb("kv1", [D, 2, ROWS])
        hm_sb = sb("hm_sb", [D, HEADS[1]])
        mask_i = sb("mask_i", [1, UNITS * KEYS], mybir.dt.uint8)
        mask_b = sb("mask_b", [1, UNITS * KEYS], bf16)
        ones_b = sb("ones_b", [1, ROWS], bf16)
        gains = sb("gains", [ROWS, 4])
        tg = sb("tg", [ROWS, 4])
        bo_sb = sb("bo_sb", [D, 1])
        bog = sb("bog", [D, 1])
        b1_sb = sb("b1_sb", [ROWS, EXPERTS])
        stats = sb("stats", [ROWS, PER_UNIT, 6])
        mv = sb("mv", [ROWS, 2, PER_UNIT, 2])
        ve = sb("ve", [ROWS, 2, PER_UNIT])
        rstd = sb("rstd", [ROWS, 2, PER_UNIT])
        mhalf = sb("mhalf", [ROWS, PER_UNIT])
        smax = sb("smax", [ROWS, 6, HEADS[1]])
        ssum = sb("ssum", [ROWS, 6, HEADS[1]])
        srec = sb("srec", [ROWS, 6, HEADS[1]])
        gl = sb("gl", [ROWS, PER_UNIT, EXPERTS])
        gs = sb("gs", [ROWS, PER_UNIT, EXPERTS])
        ge = sb("ge", [ROWS, PER_UNIT, EXPERTS])
        gq = sb("gq", [ROWS, PER_UNIT, EXPERTS])
        gp = sb("gp", [ROWS, PER_UNIT, EXPERTS])
        gt = sb("gt", [ROWS, PER_UNIT, EXPERTS])
        gr = sb("gr", [ROWS, PER_UNIT, EXPERTS])
        gw = sb("gw", [ROWS, 2, PER_UNIT, EXPERTS])
        go = sb("go", [ROWS, PER_UNIT, EXPERTS])
        g4 = sb("g4", [ROWS, 6, PER_UNIT])
        w0 = sb("w0", [ROWS, 2, PER_UNIT])

        BANK = [ctx.enter_context(nc.psum_tensor(f"bank{i}", [ROWS, 512], f32)) for i in range(8)]
        XT, AUX, OT, OB = BANK[0], BANK[1], BANK[6], BANK[7]

        in_small, in_ctx, in_w0 = sem("in_small"), sem("in_ctx"), sem("in_w0")
        in_x = [sem(f"in_x{u}") for u in range(UNITS)]
        in_w1 = sem("in_w1")
        in_ew = [sem("in_ew_even"), sem("in_ew_odd")]
        raw_rounded, raw_split = sem("raw_rounded"), sem("raw_split")
        consts = sem("consts")
        tanh_done, bog_done, mask_done = sem("tanh_done"), sem("bog_done"), sem("mask_done")
        k0_ps, v0_ps, k0_sb, v0_sb = sem("k0_ps"), sem("v0_ps"), sem("k0_sb"), sem("v0_sb")
        kv1_ps, kv1_done, kvb_done = sem("kv1_ps"), sem("kv1_done"), sem("kvb_done")
        g_ps = [sem(f"g{i}_ps") for i in range(2)]
        g_hi = [sem(f"g{i}_hi_done") for i in range(2)]
        g_lo = [sem(f"g{i}_lo_done") for i in range(2)]
        vw_ps = [sem(f"vw{i}_ps") for i in range(2)]
        vw_sb = [sem(f"vw{i}_sb") for i in range(2)]
        ln_step, ln_var, ln_rstd, xn_done = sem("ln_step"), sem("ln_var"), sem("ln_rstd"), sem("xn_done")
        xt_ps, xt_hi, xt_lo = sem("xt_ps"), sem("xt_hi_done"), sem("xt_lo_done")
        s_ps = [sem(f"scores{i}_ps") for i in range(2)]
        s_sb = [sem(f"scores{i}_sb") for i in range(2)]
        s_max = [sem(f"scores{i}_max") for i in range(2)]
        s_sub = [sem(f"scores{i}_shifted") for i in range(2)]
        p_exp = [sem(f"probs{i}_exp") for i in range(2)]
        p_sum = [sem(f"probs{i}_sum") for i in range(2)]
        p_rec = [sem(f"probs{i}_rec") for i in range(2)]
        p_norm = [sem(f"probs{i}_norm") for i in range(2)]
        pt_ps = [sem(f"probsT{i}_ps") for i in range(2)]
        pt_sb = [sem(f"probsT{i}_sb") for i in range(2)]
        o_ps = [sem(f"out{s}_ps") for s in range(4)]
        o_sb = [sem(f"out{s}_sb") for s in range(4)]
        b_ps = [sem(f"back{s}_ps") for s in range(4)]
        x_new = [sem(f"x_new{s}") for s in range(4)]
        h0_ps, h0_hi, h0_lo = sem("h0_ps"), sem("h0_hi"), sem("h0_lo")
        gate_ps, gate_sb, gate_step = sem("gate_ps"), sem("gate_sb"), sem("gate_step")
        gate_sub, gate_exp, w1_done = sem("gate_sub"), sem("gate_exp"), sem("w1_done")
        wT_ps, wT_sb, w_out = sem("wT_ps"), sem("wT_sb"), sem("w_out")
        wb_in = [sem(f"wb_in{i}") for i in range(4)]
        h_ps, v_ps, silu_done, act_done = sem("h_ps"), sem("v_ps"), sem("silu_done"), sem("act_done")
        act_hi, act_lo = sem("act_hi_done"), sem("act_lo_done")
        shared_sb, gated_done, acc_done = sem("shared_sb"), sem("gated_done"), sem("acc_done")
        stored = sem("stored")

        def xt(u):
            return slice(u * UTOK, (u + 1) * UTOK)

        def heads_of(view, n):
            return view.rearrange("p (h j) -> p h j", h=n)

        LAG_SUM, LAG_PT, LAG_AV, LAG_OT, LAG_BACK = 2, 4, 5, 5, 6
        STEPS = TILES + LAG_BACK + 1

        def unit_ends(t):
            return 0 <= t < TILES and t % PER_UNIT == PER_UNIT - 1

        NG = (1 + EXPERTS) * NCH
        AHEAD, LAST_AT, BACK_AT, RES_AT, EDGE = 2, 1, 2, 4, 5
        HBANK = (BANK[2], BANK[4], BANK[0])
        VBANK = (BANK[3], BANK[5], BANK[1])

        block = ctx.enter_context(nc.Block())

        @block.sync
        def _(sp):
            sp.dma_start(ctx_sb[:], ctx_t).then_inc(in_ctx, 16)
            sp.dma_start(wk0_sb[0:CTX, :], wk0).then_inc(in_ctx, 16)
            sp.dma_start(X[:, 0:PER_UNIT, :], x[0]).then_inc(in_x[0], 16)
            sp.dma_start(wv0_sb[0:CTX, :], wv0).then_inc(in_ctx, 16)
            sp.dma_start(wq0_sb, wq0t).then_inc(in_w0, 16)
            sp.dma_start(wo0_sb, wo0).then_inc(in_w0, 16)
            for u in range(1, UNITS):
                sp.dma_start(X[:, u * PER_UNIT:(u + 1) * PER_UNIT, :], x[u]).then_inc(in_x[u], 16)
            sp.dma_start(ew_raw[:, 0, 0:FF0COLS], ff0).then_inc(in_ew[0], 16)
            sp.dma_start(wk1_sb[:], wk1).then_inc(in_w1, 16)
            sp.dma_start(wv1_sb[:], wv1).then_inc(in_w1, 16)
            sp.dma_start(wq1_sb[:], wq1t).then_inc(in_w1, 16)
            sp.dma_start(wo1_sb[:], wo1).then_inc(in_w1, 16)
            sp.dma_start(hm_sb[:], head_mask).then_inc(in_w1, 16)
            for n in range(1, 2 + EXPERTS):
                if n >= 2:
                    sp.wait_ge(raw_split, n - 1)
                sp.dma_start(ew_raw[:, n % 2, :], ew[n - 1]).then_inc(in_ew[n % 2], 16)
            for u in range(UNITS):
                sp.wait_ge(wT_sb, u + 1)
                sp.dma_start(gate_scratch[u * EXPERTS:(u + 1) * EXPERTS, :], wT[:]).then_inc(w_out, 16)
            sp.wait_ge(w_out, 16 * UNITS)
            for n in range(4):
                sp.dma_start(wb[:, n, :], gate_scratch[n:n + 1, :].partition_broadcast(ROWS)).then_inc(wb_in[n], 16)
            with sp.Fori(1, UNITS * EXPERTS // 4) as q:
                for n in range(4):
                    sp.wait_ge(gated_done, q * 4 + (n - 3))
                    sp.dma_start(wb[:, n, :], gate_scratch[bass.ds(q * 4 + n, 1), :].partition_broadcast(ROWS)
                                 ).then_inc(wb_in[n], 16)

        @block.gpsimd
        def _(pool):
            nc.gpsimd.memset(mhalf[:], -0.5).then_inc(consts, 1)
            nc.gpsimd.memset(ones_b[:], 1.0).then_inc(consts, 1)
            nc.gpsimd.memset(go[:], 1.0).then_inc(consts, 1)
            pool.wait_ge(consts, 3)
            nc.gpsimd.memset(go[:, :, 0:1], 0.0).then_inc(consts, 1)

            def inverse_std(q):
                pool.wait_ge(ln_var, q + 1)
                if q == 0:
                    pool.wait_ge(consts, 3)
                nc.gpsimd.tensor_tensor(rstd[:, q % 2, :], ve[:, q % 2, :], mhalf[:], ALU.pow).then_inc(ln_rstd, 1)

            def split_low(n):
                pool.wait_ge(raw_rounded, n + 1)
                if n == 0:
                    nc.gpsimd.tensor_tensor(ff0l[:], ew_raw[:, 0, 0:FF0COLS], ff0h[:].bitcast(f32),
                                            ALU.subtract).then_inc(raw_split, 1)
                else:
                    nc.gpsimd.tensor_tensor(ewl[:, n - 1, :], ew_raw[:, n % 2, :], ewh[:, n - 1, :].bitcast(f32),
                                            ALU.subtract).then_inc(raw_split, 1)

            def attention(i):
                nh = HEADS[i]
                for s in range(STEPS):
                    if s < TILES:
                        pool.wait_ge(s_max[i], s + 1)
                        v = heads_of(SC[s % 6][:, 0:nh * KEYS], nh)
                        nc.gpsimd.tensor_tensor(v, v, smax[:, s % 6, 0:nh, None].to_broadcast([ROWS, nh, KEYS]),
                                                ALU.subtract).then_inc(s_sub[i], 1)
                    t = s - LAG_SUM
                    if 0 <= t < TILES:
                        pool.wait_ge(p_rec[i], t + 1)
                        v = heads_of(SC[t % 6][:, 0:nh * KEYS], nh)
                        nc.gpsimd.tensor_tensor(v, v, srec[:, t % 6, 0:nh, None].to_broadcast([ROWS, nh, KEYS]),
                                                ALU.mult).then_inc(p_norm[i], 1)
                    if s < TILES and s % PER_UNIT == 0:
                        inverse_std(2 * i * UNITS + s // PER_UNIT + 1)
                    if i == 0 and s < TILES and s % PER_UNIT == 1:
                        split_low(1 + s // PER_UNIT)

            inverse_std(0)
            split_low(0)
            attention(0)
            pool.wait_ge(kv1_done, 1)
            pool.wait_ge(pt_ps[0], TILES)
            pool.wait_ge(o_ps[0], UNITS)
            for n, dst in ((0, KB), (1, VB)):
                for u in range(UNITS):
                    nc.gpsimd.tensor_tensor(
                        heads_of(dst[:, u, :], HEADS[1]),
                        kv1[:, n, None, u * KEYS:(u + 1) * KEYS].to_broadcast([D, HEADS[1], KEYS]),
                        hm_sb[:, :, None].to_broadcast([D, HEADS[1], KEYS]), ALU.mult).then_inc(kvb_done, 1)
            for u in range(UNITS):
                inverse_std(UNITS + u + 1)
                split_low(1 + UNITS + u)
            split_low(1 + 2 * UNITS)
            attention(1)
            for u in range(1, UNITS):
                inverse_std(3 * UNITS + u)

            pool.sem_inc(acc_done, 2)
            with pool.Fori(0, UNITS) as u:
                for e in range(EXPERTS):
                    pool.wait_ge(gated_done, u * EXPERTS + (e + 1))
                    if e == 0:
                        pool.wait_ge(shared_sb, u + 1)
                    else:
                        pool.wait_ge(acc_done, u * EXPERTS + (e + 2))
                    nc.gpsimd.tensor_tensor(acc, acc, gated[:, e % 2, :], ALU.add).then_inc(acc_done, 1)

        @block.scalar
        def _(act_e):
            act_e.dma_start(gains[:, 0:2], gx.partition_broadcast(ROWS)).then_inc(in_small, 16)
            act_e.dma_start(gains[:, 2:4], gf.partition_broadcast(ROWS)).then_inc(in_small, 16)
            act_e.dma_start(ident[:], ident_in).then_inc(in_small, 16)
            act_e.dma_start(bo_sb[:], bout).then_inc(in_small, 16)
            act_e.dma_start(b1_sb[:], bias1.partition_broadcast(ROWS)).then_inc(in_small, 16)
            act_e.dma_start(mask_i[:], mask).then_inc(in_small, 16)
            act_e.wait_ge(in_small, 96)
            nc.scalar.activation(tg[:], gains[:], ACT.Tanh).then_inc(tanh_done, 1)

            def round_high(n):
                act_e.wait_ge(in_ew[n % 2], 16 * (n // 2 + 1))
                if n == 0:
                    nc.scalar.activation(ff0h[:], ew_raw[:, 0, 0:FF0COLS], ACT.Copy).then_inc(raw_rounded, 1)
                else:
                    nc.scalar.activation(ewh[:, n - 1, :], ew_raw[:, n % 2, :], ACT.Copy).then_inc(raw_rounded, 1)

            def transposed_high(q):
                act_e.wait_ge(xt_ps, q + 1)
                nc.scalar.activation(xth[:, xt(q % UNITS)], XT[:], ACT.Copy).then_inc(xt_hi, 1)

            def attention(i):
                nh = HEADS[i]
                nch = nh // 4
                scale = float(HEAD_DIM[i]) ** -0.5
                for s in range(STEPS):
                    if s < TILES:
                        act_e.wait_ge(s_ps[i], s + 1)
                        if s >= 6:
                            act_e.wait_ge(pt_ps[i], s - 5)
                        nc.scalar.activation(SC[s % 6][:, 0:nh * KEYS], BANK[2 + s % 2][:, 0:nh * KEYS],
                                             ACT.Copy).then_inc(s_sb[i], 1)
                    t = s - 1
                    if 0 <= t < TILES:
                        act_e.wait_ge(s_sub[i], t + 1)
                        nc.scalar.activation(SC[t % 6][:, 0:nh * KEYS], SC[t % 6][:, 0:nh * KEYS], ACT.Exp,
                                             scale=scale).then_inc(p_exp[i], 1)
                    t = s - LAG_PT
                    if 0 <= t < TILES:
                        u, k = divmod(t, PER_UNIT)
                        act_e.wait_ge(pt_ps[i], t + 1)
                        if u >= 2 and k == 0:
                            act_e.wait_ge(o_ps[2 * i], u - 1)
                        nc.scalar.activation(
                            PTS[:, u % 2, 0:nch, k * ROWS:(k + 1) * ROWS],
                            BANK[4 + t % 2][:, 0:nch * ROWS].rearrange("p (c n) -> p c n", c=nch),
                            ACT.Copy).then_inc(pt_sb[i], 1)
                    t = s - LAG_OT
                    if unit_ends(t):
                        u = t // PER_UNIT
                        act_e.wait_ge(o_ps[2 * i], u + 1)
                        if u >= 1:
                            act_e.wait_ge(b_ps[2 * i], u)
                        elif i == 1:
                            act_e.wait_ge(b_ps[1], UNITS)
                        if i == 0:
                            act_e.wait_ge(bog_done, 1)
                            nc.scalar.activation(oT[:], OT[:], ACT.Identity, scale=tg[:, 0:1],
                                                 bias=bog[:, 0:1]).then_inc(o_sb[0], 1)
                        else:
                            nc.scalar.activation(oT[:], OT[:], ACT.Copy, scale=tg[:, 1:2]).then_inc(o_sb[2], 1)
                    if s < TILES and s % PER_UNIT == 2:
                        transposed_high(2 * i * UNITS + s // PER_UNIT + 1)
                    if i == 0 and s < TILES and s % PER_UNIT == 1:
                        round_high(1 + s // PER_UNIT)

            act_e.wait_ge(k0_ps, 1)
            for n in range(2):
                last = nc.scalar.activation(kT0[:, 4 * n:4 * n + 4, :],
                                            BANK[2 + n][0:64, :].rearrange("p (h n) -> p h n", h=4), ACT.Copy)
                last.then_inc(k0_sb, 1)
            transposed_high(0)
            act_e.wait_ge(g_ps[0], 1)
            for n in range(2):
                nc.scalar.activation(
                    GH[0][:].rearrange("p b (h j) -> p b h j", h=8)[:, :, 4 * n:4 * n + 4, :],
                    BANK[6 + n][:].rearrange("p (h b j) -> p b h j", h=4, b=UNITS), ACT.Copy).then_inc(g_hi[0], 1)
            act_e.wait_ge(vw_ps[0], 1)
            for n in range(2):
                nc.scalar.activation(VW[0][:, 4 * n:4 * n + 4, :],
                                     BANK[2 + n][:].rearrange("p (c n) -> p c n", c=4), ACT.Copy).then_inc(vw_sb[0], 1)
            act_e.wait_ge(kv1_ps, 1)
            nc.scalar.activation(kv1[:], BANK[4][:, 0:2 * ROWS].rearrange("p (i n) -> p i n", i=2),
                                 ACT.Copy).then_inc(kv1_done, 1)
            round_high(0)
            attention(0)

            for u in range(UNITS):
                for c in range(CH0):
                    g = u * CH0 + c
                    act_e.wait_ge(h0_ps, g + 1)
                    nc.scalar.activation(acth[:, g % 3, :], BANK[2 + g % 4][:], ACT.Relu).then_inc(h0_hi, 1)
                    if c == 2:
                        transposed_high(UNITS + u + 1)
                act_e.wait_ge(gate_sub, u + 1)
                nc.scalar.activation(ge[:], gq[:], ACT.Exp).then_inc(gate_exp, 1)
                round_high(1 + UNITS + u)
                act_e.wait_ge(o_ps[1], u + 1)
                act_e.wait_ge(b_ps[1] if u else b_ps[0], u if u else UNITS)
                nc.scalar.activation(oT[:], OT[:], ACT.Copy).then_inc(o_sb[1], 1)
            round_high(1 + 2 * UNITS)

            for u in range(UNITS):
                act_e.wait_ge(g_ps[1], u + 1)
                nc.scalar.activation(GH[1][:, u, :], BANK[2 + u][:], ACT.Copy).then_inc(g_hi[1], 1)
            for u in range(UNITS):
                act_e.wait_ge(vw_ps[1], u + 1)
                nc.scalar.activation(VW[1][:, 4 * u:4 * u + 4, :],
                                     BANK[2 + u][:].rearrange("p (c n) -> p c n", c=4), ACT.Copy).then_inc(vw_sb[1], 1)
            attention(1)

            for u in range(UNITS):
                if u >= 1:
                    transposed_high(3 * UNITS + u)
                act_e.wait_ge(gate_sub, UNITS + u + 1)
                nc.scalar.activation(ge[:], gq[:], ACT.Exp).then_inc(gate_exp, 1)
                act_e.wait_ge(wT_ps, u + 1)
                if u >= 1:
                    act_e.wait_ge(w_out, 16 * u)
                nc.scalar.activation(wT[:], AUX[0:EXPERTS, :], ACT.Copy).then_inc(wT_sb, 1)

            def experts(u, j0, j1):
                for j in range(j0, j1):
                    n, r, local = CHUNKS[j % NCH], j % 3, j % NG
                    act_e.wait_ge(h_ps, u * NG + (j + 1))
                    nc.scalar.activation(silu[0:n, r, :], HBANK[r][0:n, :], ACT.Silu).then_inc(silu_done, 1)
                    act_e.wait_ge(act_done, u * NG + (j + 1))
                    nc.scalar.activation(acth[0:n, r, :], act[0:n, r, :], ACT.Copy).then_inc(act_hi, 1)
                    if local == RES_AT:
                        act_e.wait_ge(o_ps[3], (u + j // NG) * (1 + EXPERTS) + 1)
                        nc.scalar.activation(acc, OT[:], ACT.Copy).then_inc(shared_sb, 1)
                        if j >= NG:
                            store(u)

            def store(u):
                act_e.wait_ge(x_new[3], u + 1)
                act_e.dma_start(out[bass.ds(u, 1)].rearrange("o p k d -> (o p) k d"),
                                X[:, bass.ds(u * PER_UNIT, PER_UNIT), :]).then_inc(stored, 16)

            experts(0, 0, EDGE)
            with act_e.Fori(0, UNITS - 1) as u:
                experts(u, EDGE, NG + EDGE)
            experts(UNITS - 1, EDGE, NG)
            store(UNITS - 1)
            act_e.wait_ge(stored, 16 * UNITS)

        @block.vector
        def _(dve):
            count = [0]

            def link(ins):
                count[0] += 1
                ins.then_inc(gate_step, 1)
                dve.wait_ge(gate_step, count[0])

            def norm_stats(q):
                s, u = divmod(q, UNITS)
                if s == 0:
                    dve.wait_ge(in_x[u], 16)
                else:
                    dve.wait_ge(x_new[s - 1], u + 1)
                if q >= 2:
                    dve.wait_ge(xn_done, q - 1)
                for k in range(PER_UNIT):
                    last = nc.vector.bn_stats(stats[:, k, :], X[:, u * PER_UNIT + k, :])
                last.then_inc(ln_step, 1)
                dve.wait_ge(ln_step, 2 * q + 1)
                for k in range(PER_UNIT):
                    last = nc.vector.bn_aggr(mv[:, q % 2, k, :], stats[:, k, :])
                last.then_inc(ln_step, 1)
                dve.wait_ge(ln_step, 2 * q + 2)
                nc.vector.tensor_scalar(ve[:, q % 2, :], mv[:, q % 2, :, 1], EPS, None, ALU.add).then_inc(ln_var, 1)

            def normalise(q):
                u = q % UNITS
                dve.wait_ge(ln_rstd, q + 1)
                if q >= 2:
                    dve.wait_ge(xt_ps, q - 1)
                for k in range(PER_UNIT):
                    last = nc.vector.tensor_scalar(xn[:, q % 2, k, :], X[:, u * PER_UNIT + k, :],
                                                   mv[:, q % 2, k, 0:1], rstd[:, q % 2, k:k + 1],
                                                   ALU.subtract, ALU.mult)
                last.then_inc(xn_done, 1)

            def transposed_low(q):
                dve.wait_ge(xt_hi, q + 1)
                nc.vector.tensor_tensor(xtl[:, xt(q % UNITS)], XT[:], xth[:, xt(q % UNITS)].bitcast(f32),
                                        ALU.subtract).then_inc(xt_lo, 1)

            def attention(i):
                nh = HEADS[i]
                for s in range(STEPS):
                    if s < TILES:
                        dve.wait_ge(s_sb[i], s + 1)
                        if i == 1 and s < 6:
                            dve.wait_ge(p_norm[0], TILES)
                        nc.vector.reduce_max(smax[:, s % 6, 0:nh], heads_of(SC[s % 6][:, 0:nh * KEYS], nh),
                                             AX.X).then_inc(s_max[i], 1)
                    t = s - LAG_SUM
                    if 0 <= t < TILES:
                        dve.wait_ge(p_exp[i], t + 1)
                        nc.vector.reduce_sum(ssum[:, t % 6, 0:nh], heads_of(SC[t % 6][:, 0:nh * KEYS], nh),
                                             AX.X).then_inc(p_sum[i], 1)
                        dve.wait_ge(p_sum[i], t + 1)
                        nc.vector.reciprocal(srec[:, t % 6, 0:nh], ssum[:, t % 6, 0:nh]).then_inc(p_rec[i], 1)
                    if s < TILES:
                        q = 2 * i * UNITS + s // PER_UNIT + 1
                        if s % PER_UNIT == 0:
                            norm_stats(q)
                        if s % PER_UNIT == 1:
                            normalise(q)
                        if s % PER_UNIT == 3:
                            transposed_low(q)
                    t = s - LAG_BACK
                    if unit_ends(t):
                        residual(2 * i, t // PER_UNIT)

            def residual(s, u):
                xu = X[:, u * PER_UNIT:(u + 1) * PER_UNIT, :]
                dve.wait_ge(b_ps[s], u + 1)
                nc.vector.tensor_tensor(xu, OB[:].rearrange("p (k d) -> p k d", k=PER_UNIT), xu,
                                        ALU.add).then_inc(x_new[s], 1)

            dve.wait_ge(tanh_done, 1)
            nc.vector.tensor_scalar(mask_b[:], mask_i[:], 1.0, -LOWEST_BF16, ALU.subtract,
                                    ALU.mult).then_inc(mask_done, 1)
            nc.vector.tensor_scalar(bog[:], bo_sb[:], tg[:, 0:1], None, ALU.mult).then_inc(bog_done, 1)
            norm_stats(0)
            normalise(0)
            dve.wait_ge(v0_ps, 1)
            for n in range(2):
                last = nc.vector.tensor_copy(vT0[:, 4 * n:4 * n + 4, :],
                                             BANK[4 + n][0:64, :].rearrange("p (h n) -> p h n", h=4))
            last.then_inc(v0_sb, 1)
            transposed_low(0)
            for n in range(2):
                dve.wait_ge(g_hi[0], n + 1)
                v = GL[0][:].rearrange("p b (h j) -> p b h j", h=8)[:, :, 4 * n:4 * n + 4, :]
                w = GH[0][:].bitcast(f32).rearrange("p b (h j) -> p b h j", h=8)[:, :, 4 * n:4 * n + 4, :]
                nc.vector.tensor_tensor(v, BANK[6 + n][:].rearrange("p (h b j) -> p b h j", h=4, b=UNITS), w,
                                        ALU.subtract).then_inc(g_lo[0], 1)
            attention(0)

            def sorted_logits(n, bias):
                dve.wait_ge(gate_ps, n + 1)
                if n >= 1:
                    dve.wait_ge(gate_exp, n)
                v = AUX[:, 0:PER_UNIT * EXPERTS].rearrange("p (k e) -> p k e", k=PER_UNIT)
                if bias:
                    ins = nc.vector.tensor_tensor(gl[:], v, b1_sb[:, None, :].to_broadcast([ROWS, PER_UNIT, EXPERTS]),
                                                  ALU.add)
                else:
                    ins = nc.vector.tensor_copy(gl[:], v)
                ins.then_inc(gate_sb, 1)
                dve.wait_ge(gate_sb, n + 1)
                for k in range(PER_UNIT):
                    last = nc.vector.max(gs[:, k, :], gl[:, k, :])
                link(last)

            def spread(col):
                return col.to_broadcast([ROWS, PER_UNIT, EXPERTS])

            def top_two(u):
                sorted_logits(u, False)
                nc.vector.tensor_tensor(gq[:], gs[:], spread(gs[:, :, 0:1]), ALU.subtract).then_inc(gate_sub, 1)

            def top_two_weight(u):
                dve.wait_ge(gate_exp, u + 1)
                link(nc.vector.reduce_sum(g4[:, 0, :], ge[:], AX.X))
                link(nc.vector.reciprocal(g4[:, 1, :], g4[:, 0, :]))
                link(nc.vector.tensor_tensor(gt[:, :, 0:2], ge[:, :, 0:2],
                                             g4[:, 1, :, None].to_broadcast([ROWS, PER_UNIT, 2]), ALU.mult))
                link(nc.vector.reduce_sum(g4[:, 2, :], gt[:, :, 0:2], AX.X))
                link(nc.vector.tensor_scalar(g4[:, 3, :], g4[:, 2, :], F32_EPS, None, ALU.max))
                link(nc.vector.reciprocal(g4[:, 4, :], g4[:, 3, :]))
                link(nc.vector.tensor_tensor(gp[:, :, 0:2], gt[:, :, 0:2],
                                             g4[:, 4, :, None].to_broadcast([ROWS, PER_UNIT, 2]), ALU.mult))
                link(nc.vector.reduce_sum(g4[:, 5, :], gp[:, :, 0:2], AX.X))
                link(nc.vector.tensor_scalar(w0[:, u % 2, :], g4[:, 5, :], tg[:, 2:3], None, ALU.mult))

            def weighted_residual(u):
                dve.wait_ge(b_ps[1], u + 1)
                for k in range(PER_UNIT):
                    xk = X[:, u * PER_UNIT + k, :]
                    last = nc.vector.scalar_tensor_tensor(xk, OB[:, k * ROWS:(k + 1) * ROWS], w0[:, u % 2, k:k + 1],
                                                          xk, ALU.mult, ALU.add)
                last.then_inc(x_new[1], 1)

            for u in range(UNITS):
                for c in range(CH0):
                    g = u * CH0 + c
                    dve.wait_ge(h0_hi, g + 1)
                    nc.vector.scalar_tensor_tensor(actl[:, g % 3, :], BANK[2 + g % 4][:], 0.0,
                                                   acth[:, g % 3, :].bitcast(f32), ALU.max,
                                                   ALU.subtract).then_inc(h0_lo, 1)
                    if c == 0:
                        norm_stats(UNITS + u + 1)
                    if c == 1:
                        normalise(UNITS + u + 1)
                    if c == 2:
                        transposed_low(UNITS + u + 1)
                top_two(u)
                top_two_weight(u)
                if u >= 1:
                    pass
                weighted_residual(u)

            for u in range(UNITS):
                dve.wait_ge(g_hi[1], u + 1)
                nc.vector.tensor_tensor(GL[1][:, u, :], BANK[2 + u][:], GH[1][:, u, :].bitcast(f32),
                                        ALU.subtract).then_inc(g_lo[1], 1)
            attention(1)

            def top_four(u):
                sorted_logits(UNITS + u, True)
                nc.vector.tensor_tensor(gq[:], gl[:], spread(gs[:, :, 0:1]), ALU.subtract).then_inc(gate_sub, 1)
                link(nc.vector.tensor_tensor(gt[:], gl[:], spread(gs[:, :, 3:4]), ALU.is_gt))
                link(nc.vector.tensor_tensor(gp[:], gl[:], spread(gs[:, :, 3:4]), ALU.is_equal))
                link(nc.vector.reduce_sum(g4[:, 0, :], gt[:], AX.X))
                link(nc.vector.tensor_tensor_scan(gr[:].rearrange("p k e -> p (k e)"),
                                                  go[:].rearrange("p k e -> p (k e)"),
                                                  gp[:].rearrange("p k e -> p (k e)"), 0.0, ALU.mult, ALU.add))
                link(nc.vector.tensor_tensor(gr[:], gr[:], spread(g4[:, 0, :, None]), ALU.add))
                link(nc.vector.scalar_tensor_tensor(gr[:], gr[:], 4.0, gp[:], ALU.is_le, ALU.mult))
                link(nc.vector.tensor_tensor(gt[:], gt[:], gr[:], ALU.add))
                dve.wait_ge(gate_exp, UNITS + u + 1)
                link(nc.vector.tensor_tensor(gp[:], ge[:], gt[:], ALU.mult))
                link(nc.vector.reduce_sum(g4[:, 1, :], gp[:], AX.X))
                link(nc.vector.reciprocal(g4[:, 2, :], g4[:, 1, :]))
                if u >= 2:
                    dve.wait_ge(wT_ps, u - 1)
                nc.vector.tensor_tensor(gw[:, u % 2], gp[:], spread(g4[:, 2, :, None]), ALU.mult).then_inc(w1_done, 1)

            top_four(0)
            for u in range(1, UNITS):
                norm_stats(3 * UNITS + u)
                normalise(3 * UNITS + u)
                transposed_low(3 * UNITS + u)
                top_four(u)

            def gate_output(u, e):
                dve.wait_ge(o_ps[3], u * (1 + EXPERTS) + (e + 1))
                dve.wait_ge(wb_in[(e - 1) % 4], (u * 2 + (e - 1) // 4 + 1) * 16)
                dve.wait_ge(acc_done, u * EXPERTS + e)
                nc.vector.tensor_tensor(gated[:, (e - 1) % 2, :], OT[:], wb[:, (e - 1) % 4, :],
                                        ALU.mult).then_inc(gated_done, 1)

            def expert_residual(u):
                dve.wait_ge(b_ps[3], u + 1)
                xu = X[:, bass.ds(u * PER_UNIT, PER_UNIT), :]
                nc.vector.scalar_tensor_tensor(xu, OB[:].rearrange("p (k d) -> p k d", k=PER_UNIT), tg[:, 3:4], xu,
                                               ALU.mult, ALU.add).then_inc(x_new[3], 1)

            def experts(u, j0, j1):
                for j in range(j0, j1):
                    n, r, local = CHUNKS[j % NCH], j % 3, j % NG
                    dve.wait_ge(v_ps, u * NG + (j + 1))
                    dve.wait_ge(silu_done, u * NG + (j + 1))
                    nc.vector.tensor_tensor(act[0:n, r, :], silu[0:n, r, :], VBANK[r][0:n, :],
                                            ALU.mult).then_inc(act_done, 1)
                    if local == LAST_AT and j >= NG:
                        gate_output(u, EXPERTS)
                    if local == RES_AT and j >= NG:
                        expert_residual(u)
                    if local % NCH == RES_AT % NCH and local > RES_AT:
                        gate_output(u, (local - RES_AT) // NCH)
                    dve.wait_ge(act_hi, u * NG + (j + 1))
                    nc.vector.tensor_tensor(actl[0:n, r, :], act[0:n, r, :], acth[0:n, r, :].bitcast(f32),
                                            ALU.subtract).then_inc(act_lo, 1)

            experts(0, 0, EDGE)
            with dve.Fori(0, UNITS - 1) as u:
                experts(u, EDGE, NG + EDGE)
            experts(UNITS - 1, EDGE, NG)
            gate_output(UNITS - 1, EXPERTS)
            expert_residual(UNITS - 1)

        @block.tensor
        def _(pe):
            def product(out_, hi_lo, moving):
                (h, l), (mh, ml) = hi_lo, moving
                nc.tensor.matmul(out_, h, mh, start=True, stop=False)
                nc.tensor.matmul(out_, h, ml, start=False, stop=False)
                return nc.tensor.matmul(out_, l, mh, start=False, stop=True)

            def transpose_x(q):
                pe.wait_ge(xn_done, q + 1)
                if q >= 1:
                    pe.wait_ge(xt_lo, q)
                for k in range(PER_UNIT):
                    last = nc.tensor.transpose(XT[:, k * ROWS:(k + 1) * ROWS], xn[:, q % 2, k, :], ident[:])
                last.then_inc(xt_ps, 1)

            def transpose_back(s, u, src):
                if u >= 1:
                    pe.wait_ge(x_new[s], u)
                elif s >= 1:
                    pe.wait_ge(x_new[s - 1], UNITS)
                for k in range(PER_UNIT):
                    last = nc.tensor.transpose(OB[:, k * ROWS:(k + 1) * ROWS], src[:, k * ROWS:(k + 1) * ROWS],
                                               ident[:])
                last.then_inc(b_ps[s], 1)

            def attention(i):
                nh = HEADS[i]
                nch, cols = nh // 4, nh * KEYS
                for s in range(STEPS):
                    if s < TILES:
                        u = s // PER_UNIT
                        if s % PER_UNIT == 0:
                            pe.wait_ge(xt_lo, 2 * i * UNITS + u + 1)
                        if s >= 2:
                            pe.wait_ge(s_sb[i], s - 1)
                        tok = slice(s * ROWS, (s + 1) * ROWS)
                        bank = BANK[2 + s % 2][:, 0:cols]
                        nc.tensor.matmul(bank, xth[:, tok], GH[i][:, u, :], start=True, stop=False)
                        nc.tensor.matmul(bank, xth[:, tok], GL[i][:, u, :], start=False, stop=False)
                        last = nc.tensor.matmul(bank, xtl[:, tok], GH[i][:, u, :], start=False, stop=(i == 0))
                        if i == 1:
                            last = nc.tensor.matmul(
                                bank, ones_b[:],
                                mask_b[:, u * KEYS:(u + 1) * KEYS].rearrange("p (h j) -> p h j", h=1).to_broadcast([1, nh, KEYS]),
                                start=False, stop=True)
                        last.then_inc(s_ps[i], 1)
                    t = s - LAG_PT
                    if 0 <= t < TILES:
                        pe.wait_ge(p_norm[i], t + 1)
                        if t >= 2:
                            pe.wait_ge(pt_sb[i], t - 1)
                        for c in range(nch):
                            last = nc.tensor.transpose(BANK[4 + t % 2][:, c * ROWS:(c + 1) * ROWS],
                                                       SC[t % 6][:, c * ROWS:(c + 1) * ROWS], ident[:])
                        last.then_inc(pt_ps[i], 1)
                    t = s - LAG_AV
                    if unit_ends(t):
                        u = t // PER_UNIT
                        pe.wait_ge(pt_sb[i], t + 1)
                        if u >= 1:
                            pe.wait_ge(o_sb[2 * i], u)
                        elif i == 1:
                            pe.wait_ge(o_sb[1], UNITS)
                        for c in range(nch):
                            last = nc.tensor.matmul(OT[:], VW[i][:, u * nch + c, :], PTS[:, u % 2, c, :],
                                                    start=(c == 0), stop=(c == nch - 1))
                        last.then_inc(o_ps[2 * i], 1)
                    t = s - LAG_BACK
                    if unit_ends(t):
                        pe.wait_ge(o_sb[2 * i], t // PER_UNIT + 1)
                        transpose_back(2 * i, t // PER_UNIT, oT)
                    if s < TILES and s % PER_UNIT == 2:
                        transpose_x(2 * i * UNITS + s // PER_UNIT + 1)

            pe.wait_ge(in_ctx, 48)
            for w, first, done in ((wk0_sb, 2, k0_ps), (wv0_sb, 4, v0_ps)):
                for h in range(HEADS[0]):
                    last = nc.tensor.matmul(BANK[first + h // 4][0:64, (h % 4) * ROWS:(h % 4 + 1) * ROWS],
                                            w[0:CTX, h * 64:(h + 1) * 64], ctx_sb[:], start=True, stop=True)
                last.then_inc(done, 1)
            pe.wait_ge(in_small, 96)
            transpose_x(0)
            pe.wait_ge(in_w0, 32)
            pe.wait_ge(k0_sb, 2)
            for h in range(HEADS[0]):
                last = nc.tensor.matmul(BANK[6 + h // 4][:, (h % 4) * ROWS:(h % 4 + 1) * ROWS], wq0_sb[:, h, :],
                                        kT0[:, h, :], start=True, stop=True)
            last.then_inc(g_ps[0], 1)
            pe.wait_ge(v0_sb, 1)
            for u in range(UNITS):
                for c in range(2):
                    for h in range(4):
                        n = (u % 2) * 2 + c
                        last = nc.tensor.matmul(BANK[2 + u // 2][h * KEYS:(h + 1) * KEYS, n * ROWS:(n + 1) * ROWS],
                                                vT0[:, c * 4 + h, u * KEYS:(u + 1) * KEYS],
                                                wo0_sb[:, c * 4 + h, :], start=True, stop=True)
            last.then_inc(vw_ps[0], 1)
            pe.wait_ge(in_w1, 80)
            for n, w in enumerate((wk1_sb, wv1_sb)):
                last = nc.tensor.matmul(BANK[4][:, n * ROWS:(n + 1) * ROWS], w[:], ctx_sb[:], start=True, stop=True)
            last.then_inc(kv1_ps, 1)

            pe.wait_ge(g_lo[0], 2)
            pe.wait_ge(vw_sb[0], 2)
            pe.wait_ge(kv1_done, 1)
            attention(0)

            def up0(g):
                u, c = divmod(g, CH0)
                if c == 0:
                    pe.wait_ge(xt_lo, UNITS + u + 1)
                if g == 0:
                    pe.wait_ge(raw_split, 1)
                    pe.wait_ge(s_sb[0], TILES)
                    pe.wait_ge(pt_sb[0], TILES)
                if g >= 4:
                    pe.wait_ge(h0_lo, g - 3)
                w = slice(c * ROWS, (c + 1) * ROWS)
                product(BANK[2 + g % 4][:], (ff0h[:, w], ff0l[:, w]), (xth[:, xt(u)], xtl[:, xt(u)])).then_inc(h0_ps, 1)

            def down0(g):
                u, c = divmod(g, CH0)
                pe.wait_ge(h0_lo, g + 1)
                if c == 0:
                    pe.wait_ge(o_sb[1] if u else o_sb[0], u if u else UNITS)
                w = slice(DFF0 + c * D, DFF0 + (c + 1) * D)
                nc.tensor.matmul(OT[:], ff0h[:, w], acth[:, g % 3, :], start=(c == 0), stop=False)
                nc.tensor.matmul(OT[:], ff0h[:, w], actl[:, g % 3, :], start=False, stop=False)
                return nc.tensor.matmul(OT[:], ff0l[:, w], acth[:, g % 3, :], start=False, stop=(c == CH0 - 1))

            def gate_logits(n):
                i, u = divmod(n, UNITS)
                if 0 < n <= UNITS:
                    pe.wait_ge(gate_sb, n)
                elif n > UNITS:
                    pe.wait_ge(wT_sb, u)
                w = slice(DFF0 + CH0 * D + i * EXPERTS, DFF0 + CH0 * D + (i + 1) * EXPERTS)
                for k in range(PER_UNIT):
                    tok = slice(u * UTOK + k * ROWS, u * UTOK + (k + 1) * ROWS)
                    last = product(AUX[:, k * EXPERTS:(k + 1) * EXPERTS], (xth[:, tok], xtl[:, tok]),
                                   (ff0h[:, w], ff0l[:, w]))
                last.then_inc(gate_ps, 1)

            for g in range(3):
                up0(g)
            for g in range(UNITS * CH0):
                u, c = divmod(g, CH0)
                last = down0(g)
                if c == 0:
                    gate_logits(u)
                    transpose_x(UNITS + u + 1)
                if g + 3 < UNITS * CH0:
                    up0(g + 3)
                if c == CH0 - 1:
                    last.then_inc(o_ps[1], 1)
                    pe.wait_ge(o_sb[1], u + 1)
                    transpose_back(1, u, oT)

            pe.wait_ge(kvb_done, 2 * UNITS)
            pe.wait_ge(h0_lo, UNITS * CH0)
            for u in range(UNITS):
                nc.tensor.matmul(BANK[2 + u][:], wq1_sb[:], KB[:, u, :], start=True, stop=True).then_inc(g_ps[1], 1)
            for u in range(UNITS):
                pe.wait_ge(g_lo[1], u + 1)
                for c in range(4):
                    last = nc.tensor.matmul(BANK[2 + u][:, c * ROWS:(c + 1) * ROWS],
                                            VB[:, u, c * ROWS:(c + 1) * ROWS], wo1_sb[:], start=True, stop=True)
                last.then_inc(vw_ps[1], 1)
            pe.wait_ge(vw_sb[1], UNITS)
            pe.wait_ge(mask_done, 1)
            attention(1)

            for u in range(UNITS):
                if u >= 1:
                    transpose_x(3 * UNITS + u)
                pe.wait_ge(xt_lo, 3 * UNITS + u + 1)
                gate_logits(UNITS + u)
                pe.wait_ge(w1_done, u + 1)
                for k in range(PER_UNIT):
                    last = nc.tensor.transpose(AUX[0:EXPERTS, k * ROWS:(k + 1) * ROWS], gw[:, u % 2, k, :], ident[:])
                last.then_inc(wT_ps, 1)

            def up(u, j):
                e, c = divmod(j % NG, NCH)
                r, n = j % 3, CHUNKS[c]
                tok = bass.ds((u + j // NG) * UTOK, UTOK)
                xs = (xth[:, tok], xtl[:, tok])
                if not (isinstance(u, int) and u * NG + j < 3):
                    pe.wait_ge(act_done, u * NG + (j - 2))
                for k, (bank, done) in enumerate(((HBANK[r], h_ps), (VBANK[r], v_ps))):
                    w = slice(k * HID + c * ROWS, k * HID + c * ROWS + n)
                    product(bank[0:n, :], (ewh[:, e, w], ewl[:, e, w]), xs).then_inc(done, 1)

            def down(u, j):
                e, c = divmod(j % NG, NCH)
                r, n = j % 3, CHUNKS[c]
                pe.wait_ge(act_lo, u * NG + (j + 1))
                if c == 0:
                    if e == 1:
                        pe.wait_ge(shared_sb, u + (1 + j // NG))
                    elif e > 1:
                        pe.wait_ge(gated_done, u * EXPERTS + (e - 1))
                    elif j >= NG:
                        pe.wait_ge(gated_done, u * EXPERTS + EXPERTS)
                    else:
                        pe.wait_ge(o_sb[2], UNITS)
                w = slice(2 * HID + c * D, 2 * HID + (c + 1) * D)
                wh, wl = ewh[0:n, e, w], ewl[0:n, e, w]
                ah, al = acth[0:n, r, :], actl[0:n, r, :]
                nc.tensor.matmul(OT[:], wh, ah, start=(c == 0), stop=False)
                nc.tensor.matmul(OT[:], wh, al, start=False, stop=False)
                last = nc.tensor.matmul(OT[:], wl, ah, start=False, stop=(c == NCH - 1))
                if c == NCH - 1:
                    last.then_inc(o_ps[3], 1)

            def experts(u, j0, j1, last_up):
                for j in range(j0, j1):
                    if j + AHEAD <= last_up:
                        up(u, j + AHEAD)
                    if j == NG + BACK_AT:
                        back(u)
                    down(u, j)

            def back(u):
                pe.wait_ge(acc_done, u * EXPERTS + (EXPERTS + 2))
                pe.wait_ge(x_new[2], UNITS)
                for k in range(PER_UNIT):
                    last = nc.tensor.transpose(OB[:, k * ROWS:(k + 1) * ROWS], acc[:, k * ROWS:(k + 1) * ROWS], ident[:])
                last.then_inc(b_ps[3], 1)

            pe.wait_ge(raw_split, 2 + EXPERTS)
            pe.wait_ge(s_sb[1], TILES)
            pe.wait_ge(pt_sb[1], TILES)
            pe.wait_ge(wT_sb, UNITS)
            for j in range(AHEAD):
                up(0, j)
            experts(0, 0, EDGE, EDGE - 1 + AHEAD)
            with pe.Fori(0, UNITS - 1) as u:
                experts(u, EDGE, NG + EDGE, NG + EDGE - 1 + AHEAD)
            experts(UNITS - 1, EDGE, NG, NG - 1)
            back(UNITS - 1)


def kernel(**inputs):
    import numpy as np
    import concourse.bacc as bacc
    from concourse.bass_utils import run_bass_kernel_spmd

    a = {k: np.asarray(v) for k, v in inputs.items()}

    def rows(w, n):
        out = np.zeros((n * ROWS, w.shape[1]), w.dtype)
        out[:w.shape[0]] = w
        return out.reshape(n, ROWS, w.shape[1]).transpose(1, 0, 2).reshape(ROWS, -1)

    def expert(w1, w2, w3):
        return np.concatenate([w1.T, w2.T, rows(w3.T, NCH)], axis=1)

    ew = [expert(a["L1_ffn_Ws1"], a["L1_ffn_Ws2"], a["L1_ffn_Ws3"])]
    ew += [expert(a["L1_ffn_W1"][e], a["L1_ffn_W2"][e], a["L1_ffn_W3"][e]) for e in range(EXPERTS)]
    arrays = {
        "x": a["x"].reshape(UNITS, PER_UNIT, ROWS, D).transpose(0, 2, 1, 3),
        "ctx_t": a["ctx_768"].reshape(UNITS * KEYS, CTX).T,
        "mask": a["mask_BxS2_bf1"].view(np.uint8).reshape(1, -1),
        "gx": a["g_xattn"].reshape(1, 2),
        "gf": a["g_ffn"].reshape(1, 2),
        "wk0": a["L0_xattn_Wk"],
        "wq0t": a["L0_xattn_Wq"].reshape(D, HEADS[0], 64).transpose(2, 1, 0),
        "wv0": a["L0_xattn_Wv"],
        "wo0": a["L0_xattn_Wout"].reshape(HEADS[0], 64, D).transpose(1, 0, 2),
        "bout": a["L0_xattn_bout"].reshape(D, 1),
        "wk1": a["L1_xattn_Wk"],
        "wq1t": a["L1_xattn_Wq"].T,
        "wv1": a["L1_xattn_Wv"],
        "wo1": a["L1_xattn_Wo"],
        "head_mask": np.repeat(np.eye(HEADS[1], dtype=np.float32), HEAD_DIM[1], axis=0),
        "ff0": np.concatenate([a["L0_ffn_w1"], rows(a["L0_ffn_w2"], CH0), a["L0_ffn_Wg"], a["L1_ffn_Wg"].T], axis=1),
        "ew": np.stack(ew),
        "bias1": a["L1_ffn_routing_bias"].reshape(1, EXPERTS),
        "ident_in": np.eye(ROWS, dtype=np.float32),
    }
    arrays = {k: np.ascontiguousarray(v) for k, v in arrays.items()}
    nc = bacc.Bacc("TRN2", target_bir_lowering=False, num_devices=1)
    args = {k: nc.dram_tensor(k + "_dram", v.shape, mybir.dt.from_np(v.dtype), kind="ExternalInput").ap()
            for k, v in arrays.items()}
    scratch = nc.dram_tensor("gate_scratch", (UNITS * EXPERTS, UTOK), mybir.dt.float32, kind="Internal").ap()
    out = nc.dram_tensor("out_dram", (UNITS, ROWS, PER_UNIT, D), mybir.dt.float32, kind="ExternalOutput").ap()
    flamingo_kernel(nc, **args, gate_scratch=scratch, out=out)
    r = run_bass_kernel_spmd(nc, [{k + "_dram": v for k, v in arrays.items()}], core_ids=[0])
    got = np.asarray(r.results[0]["out_dram"])
    return np.ascontiguousarray(got.transpose(0, 2, 1, 3)).reshape(UNITS, UTOK, D)
```

```python
import concourse.bass as bass
from concourse import mybir
from contextlib import ExitStack

ROWS, D = 128, 128
UNITS, TILES = 4, 16
PER_UNIT = TILES // UNITS
UTOK = ROWS * PER_UNIT
KEYS, CTX = 32, 96
HEADS = (8, 16)
HEAD_DIM = (64, 8)
DFF0 = 512
CH0 = DFF0 // ROWS
EXPERTS = 8
HID = D * 2 * 4 // 3
CHUNKS = (ROWS, ROWS, HID - 2 * ROWS)
NCH = len(CHUNKS)
ECOLS = 2 * HID + NCH * D
FF0COLS = DFF0 + CH0 * D + EXPERTS + ROWS
EPS = 1e-5
F32_EPS = 1.1920928955078125e-07
LOWEST_BF16 = -3.3895313892515355e38


def flamingo_kernel(nc, x, ctx_t, mask, gx, gf, wk0, wq0t, wv0, wo0, bout, wk1, wq1t, wv1, wo1,
                    head_mask, ff0, ew, bias1, ident_in, gate_scratch, out):
    f32, f32r, bf16 = mybir.dt.float32, mybir.dt.float32r, mybir.dt.bfloat16
    ALU, ACT, AX = mybir.AluOpType, mybir.ActivationFunctionType, mybir.AxisListType

    ctx = ExitStack()
    with ctx:
        def sb(name, shape, dt=f32):
            return ctx.enter_context(nc.sbuf_tensor(name, shape, dt))

        def sem(name):
            return ctx.enter_context(nc.semaphore(name))

        X = sb("X", [ROWS, TILES, D])
        ident = sb("ident", [ROWS, D])
        ew_raw = sb("ew_raw", [ROWS, 2, max(ECOLS, FF0COLS)])
        ewh = sb("ewh", [ROWS, 1 + EXPERTS, ECOLS], f32r)
        ewl = sb("ewl", [ROWS, 1 + EXPERTS, ECOLS], f32r)
        ff0h = sb("ff0h", [ROWS, FF0COLS], f32r)
        ff0l = sb("ff0l", [ROWS, FF0COLS], f32r)
        GH = [sb(f"g{i}_hi", [ROWS, UNITS, HEADS[i] * KEYS], f32r) for i in range(2)]
        GL = [sb(f"g{i}_lo", [ROWS, UNITS, HEADS[i] * KEYS], f32r) for i in range(2)]
        VW = [sb(f"vw{i}", [ROWS, UNITS * HEADS[i] // 4, D]) for i in range(2)]
        xth = sb("xt_hi", [ROWS, UNITS * UTOK], f32r)
        xtl = sb("xt_lo", [ROWS, UNITS * UTOK], f32r)
        acth = sb("act_hi", [ROWS, 3, UTOK], f32r)
        actl = sb("act_lo", [ROWS, 3, UTOK], f32r)
        xn = sb("xn", [ROWS, 2, PER_UNIT, D])
        oT = sb("oT", [ROWS, UTOK])
        wT = oT[0:EXPERTS, :]
        glT = xn[0:EXPERTS, 1].rearrange("p k d -> p (k d)")
        arena = sb("arena", [ROWS, 14 * UTOK])
        SC = [arena[:, UTOK * i:UTOK * (i + 1)] for i in range(6)]
        PTS = arena[:, 6 * UTOK:14 * UTOK].rearrange("p (i c n) -> p i c n", i=2, c=4)
        wk0_sb, wv0_sb = SC[4], SC[5]
        big = arena[:, 6 * UTOK:14 * UTOK].rearrange("p (i h n) -> p i h n", i=4, h=8)
        wq0_sb, wo0_sb, kT0, vT0 = (big[0:64, i] for i in range(4))
        PT = [PTS[:, t // 4, t % 4].rearrange("p (c n) -> p c n", c=4) for t in range(8)]
        KB = PTS[:, 0]
        VB = PTS[:, 1]
        silu = arena[:, 0:3 * UTOK].rearrange("p (i n) -> p i n", i=3)
        act = arena[:, 3 * UTOK:6 * UTOK].rearrange("p (i n) -> p i n", i=3)
        acc = arena[:, 6 * UTOK:7 * UTOK]
        gated = arena[:, 8 * UTOK:10 * UTOK].rearrange("p (i n) -> p i n", i=2)
        wb = arena[:, 10 * UTOK:14 * UTOK].rearrange("p (i n) -> p i n", i=4)
        ctx_sb = sb("ctx_sb", [CTX, ROWS])
        wk1_sb, wv1_sb = sb("wk1_sb", [CTX, D]), sb("wv1_sb", [CTX, D])
        wq1_sb, wo1_sb = sb("wq1_sb", [D, D]), sb("wo1_sb", [D, D])
        kv1 = sb("kv1", [D, 2, ROWS])
        hm_sb = sb("hm_sb", [D, HEADS[1]])
        mask_i = sb("mask_i", [1, UNITS * KEYS], mybir.dt.uint8)
        mask_b = sb("mask_b", [1, UNITS * KEYS], bf16)
        ones_b = sb("ones_b", [1, ROWS], bf16)
        gains = sb("gains", [ROWS, 4])
        tg = sb("tg", [ROWS, 4])
        bo_sb = sb("bo_sb", [1, D])
        ones_f = sb("ones_f", [1, ROWS])
        b1_sb = sb("b1_sb", [ROWS, EXPERTS])
        stats = sb("stats", [ROWS, PER_UNIT, 6])
        mv = sb("mv", [ROWS, 2, PER_UNIT, 2])
        ve = sb("ve", [ROWS, 2, PER_UNIT])
        rstd = sb("rstd", [ROWS, 2, PER_UNIT])
        mhalf = sb("mhalf", [ROWS, PER_UNIT])
        smax = sb("smax", [ROWS, 6, HEADS[1]])
        ssum = sb("ssum", [ROWS, 6, HEADS[1]])
        srec = sb("srec", [ROWS, 6, HEADS[1]])
        gl = sb("gl", [ROWS, PER_UNIT, EXPERTS])
        gs = sb("gs", [ROWS, PER_UNIT, EXPERTS])
        ge = sb("ge", [ROWS, PER_UNIT, EXPERTS])
        gq = sb("gq", [ROWS, PER_UNIT, EXPERTS])
        gp = sb("gp", [ROWS, PER_UNIT, EXPERTS])
        gt = sb("gt", [ROWS, PER_UNIT, EXPERTS])
        gr = sb("gr", [ROWS, PER_UNIT, EXPERTS])
        gw = sb("gw", [ROWS, PER_UNIT, EXPERTS])
        euler = sb("euler", [ROWS, PER_UNIT, EXPERTS])
        go = sb("go", [ROWS, PER_UNIT, EXPERTS])
        g4 = sb("g4", [ROWS, 6, PER_UNIT])
        w0 = sb("w0", [ROWS, 2, PER_UNIT])

        BANK = [ctx.enter_context(nc.psum_tensor(f"bank{i}", [ROWS, 512], f32)) for i in range(8)]
        XT, AUX, OT, OB = BANK[0], BANK[1], BANK[6], BANK[7]

        in_small, in_ctx, in_w0 = sem("in_small"), sem("in_ctx"), sem("in_w0")
        in_x = [sem(f"in_x{u}") for u in range(UNITS)]
        in_w1 = sem("in_w1")
        in_ew = [sem("in_ew_even"), sem("in_ew_odd")]
        raw_rounded, raw_split = sem("raw_rounded"), sem("raw_split")
        consts = sem("consts")
        tanh_done, mask_done = sem("tanh_done"), sem("mask_done")
        k0_ps, v0_ps, k0_sb, v0_sb = sem("k0_ps"), sem("v0_ps"), sem("k0_sb"), sem("v0_sb")
        kv1_ps, kv1_done, kvb_done = sem("kv1_ps"), sem("kv1_done"), sem("kvb_done")
        g_ps = [sem(f"g{i}_ps") for i in range(2)]
        g_hi = [sem(f"g{i}_hi_done") for i in range(2)]
        g_lo = [sem(f"g{i}_lo_done") for i in range(2)]
        vw_ps = [sem(f"vw{i}_ps") for i in range(2)]
        vw_sb = [sem(f"vw{i}_sb") for i in range(2)]
        ln_step, ln_var, ln_rstd, xn_done = sem("ln_step"), sem("ln_var"), sem("ln_rstd"), sem("xn_done")
        xt_ps, xt_hi, xt_lo = sem("xt_ps"), sem("xt_hi_done"), sem("xt_lo_done")
        s_ps = [sem(f"scores{i}_ps") for i in range(2)]
        s_sb = [sem(f"scores{i}_sb") for i in range(2)]
        s_max = [sem(f"scores{i}_max") for i in range(2)]
        s_sub = [sem(f"scores{i}_shifted") for i in range(2)]
        p_exp = [sem(f"probs{i}_exp") for i in range(2)]
        p_sum = [sem(f"probs{i}_sum") for i in range(2)]
        p_rec = [sem(f"probs{i}_rec") for i in range(2)]
        p_norm = [sem(f"probs{i}_norm") for i in range(2)]
        pt_ps = [sem(f"probsT{i}_ps") for i in range(2)]
        pt_sb = [sem(f"probsT{i}_sb") for i in range(2)]
        o_ps = [sem(f"out{s}_ps") for s in range(4)]
        o1_sb = sem("out1_sb")
        b_ps = {s: sem(f"back{s}_ps") for s in (1, 3)}
        x_new = [sem(f"x_new{s}") for s in range(4)]
        h0_ps, h0_hi, h0_lo = sem("h0_ps"), sem("h0_hi"), sem("h0_lo")
        gate_ps, gate_sb, gate_step = sem("gate_ps"), sem("gate_sb"), sem("gate_step")
        glT_ps, glT_sb, gl_ps, chain = sem("glT_ps"), sem("glT_sb"), sem("gl_ps"), sem("gate_chain")
        top_sub, top_exp = sem("top_sub"), sem("top_exp")
        gate_sub, gate_exp, w1_done = sem("gate_sub"), sem("gate_exp"), sem("w1_done")
        wT_ps, wT_sb, w_out = sem("wT_ps"), sem("wT_sb"), sem("w_out")
        wb_in = [sem(f"wb_in{i}") for i in range(4)]
        h_ps, v_ps, silu_done, act_done = sem("h_ps"), sem("v_ps"), sem("silu_done"), sem("act_done")
        act_hi, act_lo = sem("act_hi_done"), sem("act_lo_done")
        shared_sb, gated_done, acc_done = sem("shared_sb"), sem("gated_done"), sem("acc_done")
        stored = sem("stored")

        def xt(u):
            return slice(u * UTOK, (u + 1) * UTOK)

        def heads_of(view, n):
            return view.rearrange("p (h j) -> p h j", h=n)

        LAG_EXP, LAG_SUM, LAG_NORM, LAG_PT, LAG_AV, LAG_RES = 1, 1, 2, 3, 4, 5
        STEPS = TILES + LAG_RES

        def unit_ends(t):
            return 0 <= t < TILES and t % PER_UNIT == PER_UNIT - 1

        NG = (1 + EXPERTS) * NCH
        AHEAD, LAST_AT, BACK_AT, RES_AT, EDGE = 2, 1, 2, 4, 5
        UP = BANK[2:5]

        def hbank(j):
            return UP[2 * j % 3]

        def vbank(j):
            return UP[(2 * j + 1) % 3]

        P_STATS, P_AGGR, P_NORM, P_XT, P_HI, P_LO = 5, 8, 9, 11, 13, 14
        P_GLT, P_GLT_SB, P_GL, P_WT, P_WT_SB = 15, 17, 17, NG + 2, NG + 4
        GATE_STEPS = (19, 20, 21, 23, 24, 26, 27, 29)
        FIRST_WT = 4
        CHAIN = 12

        block = ctx.enter_context(nc.Block())

        @block.sync
        def _(sp):
            sp.dma_start(ctx_sb[:], ctx_t).then_inc(in_ctx, 16)
            sp.dma_start(wk0_sb[0:CTX, :], wk0).then_inc(in_ctx, 16)
            sp.dma_start(X[:, 0:PER_UNIT, :], x[0]).then_inc(in_x[0], 16)
            sp.dma_start(wv0_sb[0:CTX, :], wv0).then_inc(in_ctx, 16)
            sp.dma_start(wq0_sb, wq0t).then_inc(in_w0, 16)
            sp.dma_start(wo0_sb, wo0).then_inc(in_w0, 16)
            for u in range(1, UNITS):
                sp.dma_start(X[:, u * PER_UNIT:(u + 1) * PER_UNIT, :], x[u]).then_inc(in_x[u], 16)
            sp.dma_start(ew_raw[:, 0, 0:FF0COLS], ff0).then_inc(in_ew[0], 16)
            sp.dma_start(wk1_sb[:], wk1).then_inc(in_w1, 16)
            sp.dma_start(wv1_sb[:], wv1).then_inc(in_w1, 16)
            sp.dma_start(wq1_sb[:], wq1t).then_inc(in_w1, 16)
            sp.dma_start(wo1_sb[:], wo1).then_inc(in_w1, 16)
            sp.dma_start(hm_sb[:], head_mask).then_inc(in_w1, 16)
            for n in range(1, 2 + EXPERTS):
                if n >= 2:
                    sp.wait_ge(raw_split, n - 1)
                sp.dma_start(ew_raw[:, n % 2, 0:ECOLS], ew[n - 1]).then_inc(in_ew[n % 2], 16)
            sp.wait_ge(raw_split, 1 + EXPERTS)
            for u in range(UNITS):
                sp.wait_ge(wT_sb, u + 1)
                sp.dma_start(gate_scratch[u * EXPERTS:(u + 1) * EXPERTS, :], wT).then_inc(w_out, 16)
                sp.wait_ge(w_out, (u + 1) * 16)
                for e in range(EXPERTS):
                    n = u * EXPERTS + e
                    if n >= 4:
                        sp.wait_ge(gated_done, n - 3)
                    sp.dma_start(wb[:, e % 4, :], gate_scratch[n:n + 1, :].partition_broadcast(ROWS)
                                 ).then_inc(wb_in[e % 4], 16)

        @block.gpsimd
        def _(pool):
            nc.gpsimd.memset(mhalf[:], -0.5).then_inc(consts, 1)
            nc.gpsimd.memset(ones_b[:], 1.0).then_inc(consts, 1)
            nc.gpsimd.memset(ones_f[:], 1.0).then_inc(consts, 1)
            nc.gpsimd.memset(go[:], 1.0).then_inc(consts, 1)
            nc.gpsimd.memset(euler[:], 2.718281828459045).then_inc(consts, 1)
            pool.wait_ge(consts, 5)
            nc.gpsimd.memset(go[:, :, 0:1], 0.0).then_inc(consts, 1)

            def inverse_std(q):
                pool.wait_ge(ln_var, q + 1)
                nc.gpsimd.tensor_tensor(rstd[:, q % 2, :], ve[:, q % 2, :], mhalf[:], ALU.pow).then_inc(ln_rstd, 1)

            def split_low_0(part):
                w = slice(part * (FF0COLS // 4), (part + 1) * (FF0COLS // 4))
                if part == 0:
                    pool.wait_ge(raw_rounded, 1)
                last = nc.gpsimd.tensor_tensor(ff0l[:, w], ew_raw[:, 0, w], ff0h[:, w].bitcast(f32), ALU.subtract)
                if part == 3:
                    last.then_inc(raw_split, 1)

            def split_low(n):
                pool.wait_ge(raw_rounded, n + 1)
                nc.gpsimd.tensor_tensor(ewl[:, n - 1, :], ew_raw[:, n % 2, 0:ECOLS], ewh[:, n - 1, :].bitcast(f32),
                                        ALU.subtract).then_inc(raw_split, 1)

            def attention(i):
                nh = HEADS[i]
                for s in range(TILES + LAG_NORM):
                    t = s - LAG_NORM
                    if t >= 0:
                        pool.wait_ge(p_rec[i], t + 1)
                        v = heads_of(SC[t % 6][:, 0:nh * KEYS], nh)
                        nc.gpsimd.tensor_tensor(v, v, srec[:, t % 6, 0:nh, None].to_broadcast([ROWS, nh, KEYS]),
                                                ALU.mult).then_inc(p_norm[i], 1)
                    if s < TILES:
                        pool.wait_ge(s_max[i], s + 1)
                        v = heads_of(SC[s % 6][:, 0:nh * KEYS], nh)
                        nc.gpsimd.tensor_tensor(v, v, smax[:, s % 6, 0:nh, None].to_broadcast([ROWS, nh, KEYS]),
                                                ALU.subtract).then_inc(s_sub[i], 1)
                        if s % PER_UNIT == 3:
                            q = 2 * i * UNITS + s // PER_UNIT + 2
                            if q <= 3 * UNITS:
                                inverse_std(q)
                    if i == 0 and s % PER_UNIT == 1 and s < TILES:
                        split_low_0(s // PER_UNIT)

            inverse_std(0)
            inverse_std(1)
            attention(0)
            pool.wait_ge(kv1_done, 1)
            pool.wait_ge(pt_ps[0], TILES)
            pool.wait_ge(o_ps[0], TILES)
            for n, dst in ((0, KB), (1, VB)):
                for u in range(UNITS):
                    nc.gpsimd.tensor_tensor(
                        heads_of(dst[:, u, :], HEADS[1]),
                        kv1[:, n, None, u * KEYS:(u + 1) * KEYS].to_broadcast([D, HEADS[1], KEYS]),
                        hm_sb[:, :, None].to_broadcast([D, HEADS[1], KEYS]), ALU.mult).then_inc(kvb_done, 1)
            for u in range(UNITS):
                inverse_std(UNITS + u + 2)
                split_low(1 + 2 * u)
                split_low(2 + 2 * u)
            split_low(1 + 2 * UNITS)
            attention(1)

            def gate_exp_1(n):
                pool.wait_ge(top_sub, n + 1)
                nc.gpsimd.tensor_tensor(ge[:], euler[:], gq[:], ALU.pow).then_inc(top_exp, 1)

            def add_experts(u, last):
                for e in range(EXPERTS):
                    pool.wait_ge(gated_done, u * EXPERTS + (e + 1))
                    if e == 0:
                        pool.wait_ge(shared_sb, u + 1)
                    else:
                        pool.wait_ge(acc_done, u * EXPERTS + (e + 2))
                    nc.gpsimd.tensor_tensor(acc, acc, gated[:, e % 2, :], ALU.add).then_inc(acc_done, 1)
                    if e == 0 and not last:
                        pool.wait_ge(ln_var, u + (3 * UNITS + 2))
                        nc.gpsimd.tensor_tensor(rstd[:, 0, :], ve[:, 0, :], mhalf[:], ALU.pow).then_inc(ln_rstd, 1)
                    if e == 5 and not last:
                        gate_exp_1(u + 1)

            gate_exp_1(0)
            pool.sem_inc(acc_done, 2)
            with pool.Fori(0, UNITS - 1) as u:
                add_experts(u, False)
            add_experts(UNITS - 1, True)

        @block.scalar
        def _(act_e):
            act_e.dma_start(gains[:, 0:2], gx.partition_broadcast(ROWS)).then_inc(in_small, 16)
            act_e.dma_start(gains[:, 2:4], gf.partition_broadcast(ROWS)).then_inc(in_small, 16)
            act_e.dma_start(ident[:], ident_in).then_inc(in_small, 16)
            act_e.dma_start(bo_sb[:], bout).then_inc(in_small, 16)
            act_e.dma_start(b1_sb[:], bias1.partition_broadcast(ROWS)).then_inc(in_small, 16)
            act_e.dma_start(mask_i[:], mask).then_inc(in_small, 16)
            act_e.wait_ge(in_small, 96)
            nc.scalar.activation(tg[:], gains[:], ACT.Tanh).then_inc(tanh_done, 1)

            def round_high(n):
                act_e.wait_ge(in_ew[n % 2], 16 * (n // 2 + 1))
                if n == 0:
                    nc.scalar.activation(ff0h[:], ew_raw[:, 0, 0:FF0COLS], ACT.Copy).then_inc(raw_rounded, 1)
                else:
                    nc.scalar.activation(ewh[:, n - 1, :], ew_raw[:, n % 2, 0:ECOLS], ACT.Copy).then_inc(raw_rounded, 1)

            def transposed_high(q):
                act_e.wait_ge(xt_ps, q + 1)
                nc.scalar.activation(xth[:, xt(q % UNITS)], XT[:], ACT.Copy).then_inc(xt_hi, 1)

            def attention(i):
                nh = HEADS[i]
                nch = nh // 4
                scale = float(HEAD_DIM[i]) ** -0.5
                for s in range(TILES + LAG_PT):
                    if s < TILES:
                        act_e.wait_ge(s_ps[i], s + 1)
                        if s >= 6:
                            act_e.wait_ge(pt_ps[i], s - 5)
                        nc.scalar.activation(SC[s % 6][:, 0:nh * KEYS], BANK[2 + s % 2][:, 0:nh * KEYS],
                                             ACT.Copy).then_inc(s_sb[i], 1)
                        if s % PER_UNIT == 2:
                            transposed_high(2 * i * UNITS + s // PER_UNIT + 1)
                    t = s - LAG_EXP
                    if 0 <= t < TILES:
                        act_e.wait_ge(s_sub[i], t + 1)
                        nc.scalar.activation(SC[t % 6][:, 0:nh * KEYS], SC[t % 6][:, 0:nh * KEYS], ACT.Exp,
                                             scale=scale).then_inc(p_exp[i], 1)
                    t = s - LAG_PT
                    if t >= 0:
                        act_e.wait_ge(pt_ps[i], t + 1)
                        if t >= 8:
                            act_e.wait_ge(o_ps[2 * i], t - 7)
                        nc.scalar.activation(PT[t % 8][:, 0:nch, :],
                                             BANK[4 + t % 2][:, 0:nch * ROWS].rearrange("p (c n) -> p c n", c=nch),
                                             ACT.Copy).then_inc(pt_sb[i], 1)
                    if i == 0 and s in (1, 8):
                        round_high(s // 8)

            act_e.wait_ge(k0_ps, 1)
            for n in range(2):
                last = nc.scalar.activation(kT0[:, 4 * n:4 * n + 4, :],
                                            BANK[2 + n][0:64, :].rearrange("p (h n) -> p h n", h=4), ACT.Copy)
                last.then_inc(k0_sb, 1)
            transposed_high(0)
            act_e.wait_ge(g_ps[0], 1)
            for n in range(2):
                nc.scalar.activation(
                    GH[0][:].rearrange("p b (h j) -> p b h j", h=8)[:, :, 4 * n:4 * n + 4, :],
                    BANK[6 + n][:].rearrange("p (h b j) -> p b h j", h=4, b=UNITS), ACT.Copy).then_inc(g_hi[0], 1)
            act_e.wait_ge(vw_ps[0], 1)
            for n in range(2):
                nc.scalar.activation(VW[0][:, 4 * n:4 * n + 4, :],
                                     BANK[2 + n][:].rearrange("p (c n) -> p c n", c=4), ACT.Copy).then_inc(vw_sb[0], 1)
            act_e.wait_ge(kv1_ps, 1)
            nc.scalar.activation(kv1[:], BANK[4][:, 0:2 * ROWS].rearrange("p (i n) -> p i n", i=2),
                                 ACT.Copy).then_inc(kv1_done, 1)
            attention(0)

            for u in range(UNITS):
                for c in range(CH0):
                    g = u * CH0 + c
                    act_e.wait_ge(h0_ps, g + 1)
                    nc.scalar.activation(acth[:, g % 3, :], BANK[2 + g % 4][:], ACT.Relu).then_inc(h0_hi, 1)
                    if c == 2:
                        transposed_high(UNITS + u + 1)
                    if c == 0 and u:
                        round_high(1 + 2 * u)
                act_e.wait_ge(gate_sub, u + 1)
                nc.scalar.activation(ge[:], gq[:], ACT.Exp).then_inc(gate_exp, 1)
                round_high(2 + 2 * u)
                act_e.wait_ge(o_ps[1], u + 1)
                if u >= 1:
                    act_e.wait_ge(b_ps[1], u)
                nc.scalar.activation(oT[:], OT[:], ACT.Copy).then_inc(o1_sb, 1)
            round_high(1 + 2 * UNITS)

            for u in range(UNITS):
                act_e.wait_ge(g_ps[1], u + 1)
                nc.scalar.activation(GH[1][:, u, :], BANK[2 + u][:], ACT.Copy).then_inc(g_hi[1], 1)
            for u in range(UNITS):
                act_e.wait_ge(vw_ps[1], u + 1)
                nc.scalar.activation(VW[1][:, 4 * u:4 * u + 4, :],
                                     BANK[2 + u][:].rearrange("p (c n) -> p c n", c=4), ACT.Copy).then_inc(vw_sb[1], 1)
            attention(1)

            def gate_logits_out(n):
                act_e.wait_ge(glT_ps, n + 1)
                nc.scalar.activation(glT, AUX[0:EXPERTS, :], ACT.Copy).then_inc(glT_sb, 1)

            def gate_weights_out(n):
                act_e.wait_ge(wT_ps, n + 1)
                if not isinstance(n, int):
                    act_e.wait_ge(w_out, n * 16)
                nc.scalar.activation(wT, AUX[0:EXPERTS, :], ACT.Copy).then_inc(wT_sb, 1)

            gate_logits_out(0)

            def experts(u, j0, j1):
                for j in range(j0, j1):
                    n, r, local = CHUNKS[j % NCH], j % 3, j % NG
                    act_e.wait_ge(h_ps, u * NG + (j + 1))
                    nc.scalar.activation(silu[0:n, r, :], hbank(j)[0:n, :], ACT.Silu).then_inc(silu_done, 1)
                    act_e.wait_ge(act_done, u * NG + (j + 1))
                    nc.scalar.activation(acth[0:n, r, :], act[0:n, r, :], ACT.Copy).then_inc(act_hi, 1)
                    if local == RES_AT:
                        act_e.wait_ge(o_ps[3], (u + j // NG) * (1 + EXPERTS) + 1)
                        nc.scalar.activation(acc, OT[:], ACT.Copy).then_inc(shared_sb, 1)
                        if j >= NG:
                            store(u)
                    if not isinstance(u, int):
                        if j == P_HI:
                            act_e.wait_ge(xt_ps, u + (3 * UNITS + 2))
                            nc.scalar.activation(xth[:, bass.ds((u + 1) * UTOK, UTOK)], XT[:], ACT.Copy
                                                 ).then_inc(xt_hi, 1)
                        if j == P_GLT_SB:
                            gate_logits_out(u + 1)
                        if j == P_WT_SB:
                            gate_weights_out(u + 1)
                    elif j == FIRST_WT:
                        gate_weights_out(0)

            def store(u):
                act_e.wait_ge(x_new[3], u + 1)
                act_e.dma_start(out[bass.ds(u, 1)].rearrange("o p k d -> (o p) k d"),
                                X[:, bass.ds(u * PER_UNIT, PER_UNIT), :]).then_inc(stored, 16)

            experts(0, 0, EDGE)
            with act_e.Fori(0, UNITS - 1) as u:
                experts(u, EDGE, NG + EDGE)
            experts(UNITS - 1, EDGE, NG)
            store(UNITS - 1)
            act_e.wait_ge(stored, 16 * UNITS)

        @block.vector
        def _(dve):
            count = [0]

            def link(ins):
                count[0] += 1
                ins.then_inc(gate_step, 1)
                dve.wait_ge(gate_step, count[0])

            def norm_stats(q):
                s, u = divmod(q, UNITS)
                if s == 0:
                    dve.wait_ge(in_x[u], 16)
                else:
                    dve.wait_ge(x_new[s - 1], u + 1)
                if q >= 2:
                    dve.wait_ge(xn_done, q - 1)
                for k in range(PER_UNIT):
                    last = nc.vector.bn_stats(stats[:, k, :], X[:, u * PER_UNIT + k, :])
                last.then_inc(ln_step, 1)
                dve.wait_ge(ln_step, 2 * q + 1)
                for k in range(PER_UNIT):
                    last = nc.vector.bn_aggr(mv[:, q % 2, k, :], stats[:, k, :])
                last.then_inc(ln_step, 1)
                dve.wait_ge(ln_step, 2 * q + 2)
                nc.vector.tensor_scalar(ve[:, q % 2, :], mv[:, q % 2, :, 1], EPS, None, ALU.add).then_inc(ln_var, 1)

            def normalise(q, tiles=range(PER_UNIT)):
                u = q % UNITS
                dve.wait_ge(ln_rstd, q + 1)
                if q >= 2:
                    dve.wait_ge(xt_ps, q - 1)
                for k in tiles:
                    last = nc.vector.tensor_scalar(xn[:, q % 2, k, :], X[:, u * PER_UNIT + k, :],
                                                   mv[:, q % 2, k, 0:1], rstd[:, q % 2, k:k + 1],
                                                   ALU.subtract, ALU.mult)
                if k == PER_UNIT - 1:
                    last.then_inc(xn_done, 1)

            def transposed_low(q):
                dve.wait_ge(xt_hi, q + 1)
                nc.vector.tensor_tensor(xtl[:, xt(q % UNITS)], XT[:], xth[:, xt(q % UNITS)].bitcast(f32),
                                        ALU.subtract).then_inc(xt_lo, 1)

            def attention(i):
                nh = HEADS[i]
                for s in range(STEPS):
                    q = 2 * i * UNITS + s // PER_UNIT + 1
                    if s < TILES:
                        dve.wait_ge(s_sb[i], s + 1)
                        if i == 1 and s < 6:
                            dve.wait_ge(p_norm[0], TILES)
                        nc.vector.reduce_max(smax[:, s % 6, 0:nh], heads_of(SC[s % 6][:, 0:nh * KEYS], nh),
                                             AX.X).then_inc(s_max[i], 1)
                    t = s - LAG_SUM
                    if 0 <= t < TILES:
                        dve.wait_ge(p_exp[i], t + 1)
                        nc.vector.reduce_sum(ssum[:, t % 6, 0:nh], heads_of(SC[t % 6][:, 0:nh * KEYS], nh),
                                             AX.X).then_inc(p_sum[i], 1)
                    if s < TILES and s % PER_UNIT in (0, 1):
                        normalise(q, (0, 1) if s % PER_UNIT == 0 else (2, 3))
                    if s < TILES and s % PER_UNIT == 2:
                        transposed_low(q)
                    if 0 <= t < TILES:
                        dve.wait_ge(p_sum[i], t + 1)
                        nc.vector.reciprocal(srec[:, t % 6, 0:nh], ssum[:, t % 6, 0:nh]).then_inc(p_rec[i], 1)
                    if s < TILES and s % PER_UNIT == 3 and q + 1 <= 3 * UNITS:
                        norm_stats(q + 1)
                    t = s - LAG_RES
                    if unit_ends(t):
                        residual(2 * i, t // PER_UNIT)

            def residual(s, u):
                xu = X[:, u * PER_UNIT:(u + 1) * PER_UNIT, :]
                dve.wait_ge(o_ps[s], (u + 1) * PER_UNIT)
                nc.vector.scalar_tensor_tensor(xu, BANK[6 + u % 2][:].rearrange("p (k d) -> p k d", k=PER_UNIT),
                                               tg[:, s // 2:s // 2 + 1], xu, ALU.mult, ALU.add).then_inc(x_new[s], 1)

            dve.wait_ge(tanh_done, 1)
            nc.vector.tensor_scalar(mask_b[:], mask_i[:], 1.0, -LOWEST_BF16, ALU.subtract,
                                    ALU.mult).then_inc(mask_done, 1)
            norm_stats(0)
            normalise(0)
            norm_stats(1)
            dve.wait_ge(v0_ps, 1)
            for n in range(2):
                last = nc.vector.tensor_copy(vT0[:, 4 * n:4 * n + 4, :],
                                             BANK[4 + n][0:64, :].rearrange("p (h n) -> p h n", h=4))
            last.then_inc(v0_sb, 1)
            transposed_low(0)
            for n in range(2):
                dve.wait_ge(g_hi[0], n + 1)
                v = GL[0][:].rearrange("p b (h j) -> p b h j", h=8)[:, :, 4 * n:4 * n + 4, :]
                w = GH[0][:].bitcast(f32).rearrange("p b (h j) -> p b h j", h=8)[:, :, 4 * n:4 * n + 4, :]
                nc.vector.tensor_tensor(v, BANK[6 + n][:].rearrange("p (h b j) -> p b h j", h=4, b=UNITS), w,
                                        ALU.subtract).then_inc(g_lo[0], 1)
            attention(0)

            def spread(col, n=EXPERTS):
                return col.to_broadcast([ROWS, PER_UNIT, n])

            def top_two(u, part):
                if part == 0:
                    dve.wait_ge(gate_ps, u + 1)
                    nc.vector.tensor_copy(gl[:], AUX[:, 0:PER_UNIT * EXPERTS].rearrange("p (k e) -> p k e", k=PER_UNIT)
                                          ).then_inc(gate_sb, 1)
                    dve.wait_ge(gate_sb, u + 1)
                    for k in range(PER_UNIT):
                        last = nc.vector.max(gs[:, k, :], gl[:, k, :])
                    link(last)
                    nc.vector.tensor_tensor(gq[:], gs[:], spread(gs[:, :, 0:1]), ALU.subtract).then_inc(gate_sub, 1)
                if part == 1:
                    dve.wait_ge(gate_exp, u + 1)
                    link(nc.vector.reduce_sum(g4[:, 0, :], ge[:], AX.X))
                    link(nc.vector.reciprocal(g4[:, 1, :], g4[:, 0, :]))
                    link(nc.vector.tensor_tensor(gt[:, :, 0:2], ge[:, :, 0:2], spread(g4[:, 1, :, None], 2), ALU.mult))
                if part == 2:
                    link(nc.vector.reduce_sum(g4[:, 2, :], gt[:, :, 0:2], AX.X))
                    link(nc.vector.tensor_scalar(g4[:, 3, :], g4[:, 2, :], F32_EPS, None, ALU.max))
                    link(nc.vector.reciprocal(g4[:, 4, :], g4[:, 3, :]))
                if part == 3:
                    link(nc.vector.tensor_tensor(gp[:, :, 0:2], gt[:, :, 0:2], spread(g4[:, 4, :, None], 2), ALU.mult))
                    link(nc.vector.reduce_sum(g4[:, 5, :], gp[:, :, 0:2], AX.X))
                    link(nc.vector.tensor_scalar(w0[:, u % 2, :], g4[:, 5, :], tg[:, 2:3], None, ALU.mult))

            def weighted_residual(u):
                dve.wait_ge(b_ps[1], u + 1)
                for k in range(PER_UNIT):
                    xk = X[:, u * PER_UNIT + k, :]
                    last = nc.vector.scalar_tensor_tensor(xk, OB[:, k * ROWS:(k + 1) * ROWS], w0[:, u % 2, k:k + 1],
                                                          xk, ALU.mult, ALU.add)
                last.then_inc(x_new[1], 1)

            for u in range(UNITS):
                for c in range(CH0):
                    g = u * CH0 + c
                    dve.wait_ge(h0_hi, g + 1)
                    nc.vector.scalar_tensor_tensor(actl[:, g % 3, :], BANK[2 + g % 4][:], 0.0,
                                                   acth[:, g % 3, :].bitcast(f32), ALU.max,
                                                   ALU.subtract).then_inc(h0_lo, 1)
                    if c == 0:
                        norm_stats(UNITS + u + 2)
                    if c == 1:
                        normalise(UNITS + u + 1)
                    if c == 2:
                        transposed_low(UNITS + u + 1)
                    if c == CH0 - 1:
                        top_two(u, 0)
                    elif u >= 1:
                        top_two(u - 1, 1 + c)
                        if c == 2:
                            weighted_residual(u - 1)
            for part in (1, 2, 3):
                top_two(UNITS - 1, part)
            weighted_residual(UNITS - 1)

            for u in range(UNITS):
                dve.wait_ge(g_hi[1], u + 1)
                nc.vector.tensor_tensor(GL[1][:, u, :], BANK[2 + u][:], GH[1][:, u, :].bitcast(f32),
                                        ALU.subtract).then_inc(g_lo[1], 1)
            attention(1)

            def top_four(n, part):
                def linked(ins, at):
                    ins.then_inc(chain, 1)
                    dve.wait_ge(chain, n * CHAIN + at)

                if part == 0:
                    dve.wait_ge(gl_ps, n + 1)
                    v = BANK[5][:, 0:PER_UNIT * EXPERTS].rearrange("p (k e) -> p k e", k=PER_UNIT)
                    linked(nc.vector.tensor_tensor(gl[:], v, b1_sb[:, None, :].to_broadcast([ROWS, PER_UNIT, EXPERTS]),
                                                   ALU.add), 1)
                if part == 1:
                    for k in range(PER_UNIT):
                        last = nc.vector.max(gs[:, k, :], gl[:, k, :])
                    linked(last, 2)
                if part == 2:
                    linked(nc.vector.tensor_tensor(gq[:], gl[:], spread(gs[:, :, 0:1]), ALU.subtract), 3)
                    nc.vector.tensor_tensor(gt[:], gl[:], spread(gs[:, :, 3:4]), ALU.is_gt).then_inc(top_sub, 1)
                    dve.wait_ge(top_sub, n + 1)
                if part == 3:
                    linked(nc.vector.tensor_tensor(gp[:], gl[:], spread(gs[:, :, 3:4]), ALU.is_equal), 4)
                    linked(nc.vector.reduce_sum(g4[:, 0, :], gt[:], AX.X), 5)
                if part == 4:
                    linked(nc.vector.tensor_tensor_scan(gr[:].rearrange("p k e -> p (k e)"),
                                                        go[:].rearrange("p k e -> p (k e)"),
                                                        gp[:].rearrange("p k e -> p (k e)"), 0.0, ALU.mult, ALU.add), 6)
                    linked(nc.vector.tensor_tensor(gr[:], gr[:], spread(g4[:, 0, :, None]), ALU.add), 7)
                if part == 5:
                    linked(nc.vector.scalar_tensor_tensor(gr[:], gr[:], 4.0, gp[:], ALU.is_le, ALU.mult), 8)
                    linked(nc.vector.tensor_tensor(gt[:], gt[:], gr[:], ALU.add), 9)
                if part == 6:
                    dve.wait_ge(top_exp, n + 1)
                    linked(nc.vector.tensor_tensor(gp[:], ge[:], gt[:], ALU.mult), 10)
                    linked(nc.vector.reduce_sum(g4[:, 1, :], gp[:], AX.X), 11)
                if part == 7:
                    linked(nc.vector.reciprocal(g4[:, 2, :], g4[:, 1, :]), 12)
                    if not isinstance(n, int):
                        dve.wait_ge(wT_ps, n)
                    nc.vector.tensor_tensor(gw[:], gp[:], spread(g4[:, 2, :, None]), ALU.mult).then_inc(w1_done, 1)

            def prepare(n, j):
                xu = bass.ds(n * PER_UNIT, PER_UNIT)
                if j in (P_STATS, P_STATS + 1):
                    dve.wait_ge(x_new[2], UNITS)
                    for k in (0, 1) if j == P_STATS else (2, 3):
                        last = nc.vector.bn_stats(stats[:, k, :], X[:, bass.ds(n * PER_UNIT + k, 1), :])
                    if j == P_STATS + 1:
                        last.then_inc(ln_step, 1)
                if j == P_AGGR:
                    for k in range(PER_UNIT):
                        last = nc.vector.bn_aggr(mv[:, 0, k, :], stats[:, k, :])
                    last.then_inc(ln_step, 1)
                    dve.wait_ge(ln_step, n * 2 + (6 * UNITS + 2))
                    nc.vector.tensor_scalar(ve[:, 0, :], mv[:, 0, :, 1], EPS, None, ALU.add).then_inc(ln_var, 1)
                if j in (P_NORM, P_NORM + 2):
                    dve.wait_ge(ln_rstd, n + (3 * UNITS + 1))
                    for k in (0, 1) if j == P_NORM else (2, 3):
                        last = nc.vector.tensor_scalar(xn[:, 0, k, :], X[:, bass.ds(n * PER_UNIT + k, 1), :],
                                                       mv[:, 0, k, 0:1], rstd[:, 0, k:k + 1],
                                                       ALU.subtract, ALU.mult)
                    if j == P_NORM + 2:
                        last.then_inc(xn_done, 1)
                if j == P_LO:
                    dve.wait_ge(xt_hi, n + (3 * UNITS + 1))
                    xs = bass.ds(n * UTOK, UTOK)
                    nc.vector.tensor_tensor(xtl[:, xs], XT[:], xth[:, xs].bitcast(f32), ALU.subtract).then_inc(xt_lo, 1)
                for part, at in enumerate(GATE_STEPS):
                    if j == at:
                        top_four(n, part)

            def gate_output(u, e):
                dve.wait_ge(o_ps[3], u * (1 + EXPERTS) + (e + 1))
                dve.wait_ge(wb_in[(e - 1) % 4], (u * 2 + (e - 1) // 4 + 1) * 16)
                dve.wait_ge(acc_done, u * EXPERTS + e)
                nc.vector.tensor_tensor(gated[:, (e - 1) % 2, :], OT[:], wb[:, (e - 1) % 4, :],
                                        ALU.mult).then_inc(gated_done, 1)

            def expert_residual(u):
                dve.wait_ge(b_ps[3], u + 1)
                xu = X[:, bass.ds(u * PER_UNIT, PER_UNIT), :]
                nc.vector.scalar_tensor_tensor(xu, OB[:].rearrange("p (k d) -> p k d", k=PER_UNIT), tg[:, 3:4], xu,
                                               ALU.mult, ALU.add).then_inc(x_new[3], 1)

            def experts(u, j0, j1):
                for j in range(j0, j1):
                    n, r, local = CHUNKS[j % NCH], j % 3, j % NG
                    dve.wait_ge(v_ps, u * NG + (j + 1))
                    dve.wait_ge(silu_done, u * NG + (j + 1))
                    if j == P_AGGR and not isinstance(u, int):
                        dve.wait_ge(ln_step, u * 2 + (6 * UNITS + 3))
                    nc.vector.tensor_tensor(act[0:n, r, :], silu[0:n, r, :], vbank(j)[0:n, :],
                                            ALU.mult).then_inc(act_done, 1)
                    if local == LAST_AT and j >= NG:
                        gate_output(u, EXPERTS)
                    if local == RES_AT and j >= NG:
                        expert_residual(u)
                    if local % NCH == RES_AT % NCH and local > RES_AT:
                        gate_output(u, (local - RES_AT) // NCH)
                    if not isinstance(u, int):
                        prepare(u + 1, j)
                    elif j < FIRST_WT:
                        top_four(0, 2 * j)
                        top_four(0, 2 * j + 1)
                    dve.wait_ge(act_hi, u * NG + (j + 1))
                    nc.vector.tensor_tensor(actl[0:n, r, :], act[0:n, r, :], acth[0:n, r, :].bitcast(f32),
                                            ALU.subtract).then_inc(act_lo, 1)

            experts(0, 0, EDGE)
            with dve.Fori(0, UNITS - 1) as u:
                experts(u, EDGE, NG + EDGE)
            experts(UNITS - 1, EDGE, NG)
            gate_output(UNITS - 1, EXPERTS)
            expert_residual(UNITS - 1)

        @block.tensor
        def _(pe):
            def product(out_, hi_lo, moving):
                (h, l), (mh, ml) = hi_lo, moving
                nc.tensor.matmul(out_, h, mh, start=True, stop=False)
                nc.tensor.matmul(out_, h, ml, start=False, stop=False)
                return nc.tensor.matmul(out_, l, mh, start=False, stop=True)

            def transpose_x(q):
                pe.wait_ge(xn_done, q + 1)
                if q >= 1:
                    pe.wait_ge(xt_lo, q)
                for k in range(PER_UNIT):
                    last = nc.tensor.transpose(XT[:, k * ROWS:(k + 1) * ROWS], xn[:, q % 2, k, :], ident[:])
                last.then_inc(xt_ps, 1)

            def transpose_back(u):
                pe.wait_ge(o1_sb, u + 1)
                if u >= 1:
                    pe.wait_ge(x_new[1], u)
                else:
                    pe.wait_ge(x_new[0], UNITS)
                for k in range(PER_UNIT):
                    last = nc.tensor.transpose(OB[:, k * ROWS:(k + 1) * ROWS], oT[:, k * ROWS:(k + 1) * ROWS],
                                               ident[:])
                last.then_inc(b_ps[1], 1)

            def attention(i, begin_next):
                nh = HEADS[i]
                nch, cols = nh // 4, nh * KEYS
                for s in range(TILES + LAG_AV):
                    if s < TILES:
                        u = s // PER_UNIT
                        if s % PER_UNIT == 0:
                            pe.wait_ge(xt_lo, 2 * i * UNITS + u + 1)
                        if s >= 2:
                            pe.wait_ge(s_sb[i], s - 1)
                        tok = slice(s * ROWS, (s + 1) * ROWS)
                        bank = BANK[2 + s % 2][:, 0:cols]
                        nc.tensor.matmul(bank, xth[:, tok], GH[i][:, u, :], start=True, stop=False)
                        nc.tensor.matmul(bank, xth[:, tok], GL[i][:, u, :], start=False, stop=False)
                        last = nc.tensor.matmul(bank, xtl[:, tok], GH[i][:, u, :], start=False, stop=(i == 0))
                        if i == 1:
                            last = nc.tensor.matmul(
                                bank, ones_b[:],
                                mask_b[:, u * KEYS:(u + 1) * KEYS].rearrange("p (h j) -> p h j", h=1).to_broadcast([1, nh, KEYS]),
                                start=False, stop=True)
                        last.then_inc(s_ps[i], 1)
                    t = s - LAG_PT
                    if 0 <= t < TILES:
                        pe.wait_ge(p_norm[i], t + 1)
                        if t >= 2:
                            pe.wait_ge(pt_sb[i], t - 1)
                        for c in range(nch):
                            last = nc.tensor.transpose(BANK[4 + t % 2][:, c * ROWS:(c + 1) * ROWS],
                                                       SC[t % 6][:, c * ROWS:(c + 1) * ROWS], ident[:])
                        last.then_inc(pt_ps[i], 1)
                    t = s - LAG_AV
                    if 0 <= t < TILES:
                        u, k = divmod(t, PER_UNIT)
                        pe.wait_ge(pt_sb[i], t + 1)
                        if k == 0 and u >= 2:
                            pe.wait_ge(x_new[2 * i], u - 1)
                        elif t == 0 and i == 1:
                            pe.wait_ge(x_new[1], UNITS)
                        o = BANK[6 + u % 2][:, k * ROWS:(k + 1) * ROWS]
                        if i == 0:
                            nc.tensor.matmul(o, ones_f[:], bo_sb[:], start=True, stop=False)
                        for c in range(nch):
                            last = nc.tensor.matmul(o, PT[t % 8][:, c, :], VW[i][:, u * nch + c, :],
                                                    start=(i == 1 and c == 0), stop=(c == nch - 1))
                        last.then_inc(o_ps[2 * i], 1)
                    if s < TILES and s % PER_UNIT == 1:
                        transpose_x(2 * i * UNITS + s // PER_UNIT + 1)
                    if s >= TILES + LAG_AV - 3:
                        begin_next(s - (TILES + LAG_AV - 3))

            pe.wait_ge(in_ctx, 48)
            for w, first, done in ((wk0_sb, 2, k0_ps), (wv0_sb, 4, v0_ps)):
                for h in range(HEADS[0]):
                    last = nc.tensor.matmul(BANK[first + h // 4][0:64, (h % 4) * ROWS:(h % 4 + 1) * ROWS],
                                            w[0:CTX, h * 64:(h + 1) * 64], ctx_sb[:], start=True, stop=True)
                last.then_inc(done, 1)
            pe.wait_ge(in_small, 96)
            transpose_x(0)
            pe.wait_ge(in_w0, 32)
            pe.wait_ge(k0_sb, 2)
            for h in range(HEADS[0]):
                last = nc.tensor.matmul(BANK[6 + h // 4][:, (h % 4) * ROWS:(h % 4 + 1) * ROWS], wq0_sb[:, h, :],
                                        kT0[:, h, :], start=True, stop=True)
            last.then_inc(g_ps[0], 1)
            pe.wait_ge(v0_sb, 1)
            for u in range(UNITS):
                for c in range(2):
                    for h in range(4):
                        n = (u % 2) * 2 + c
                        last = nc.tensor.matmul(BANK[2 + u // 2][h * KEYS:(h + 1) * KEYS, n * ROWS:(n + 1) * ROWS],
                                                vT0[:, c * 4 + h, u * KEYS:(u + 1) * KEYS],
                                                wo0_sb[:, c * 4 + h, :], start=True, stop=True)
            last.then_inc(vw_ps[0], 1)
            pe.wait_ge(in_w1, 80)
            for n, w in enumerate((wk1_sb, wv1_sb)):
                last = nc.tensor.matmul(BANK[4][:, n * ROWS:(n + 1) * ROWS], w[:], ctx_sb[:], start=True, stop=True)
            last.then_inc(kv1_ps, 1)


            def up0(g):
                u, c = divmod(g, CH0)
                if c == 0:
                    pe.wait_ge(xt_lo, UNITS + u + 1)
                if g == 0:
                    pe.wait_ge(raw_split, 1)
                    pe.wait_ge(s_sb[0], TILES)
                if g in (2, 3):
                    pe.wait_ge(pt_sb[0], TILES - 3 + g)
                if g >= 4:
                    pe.wait_ge(h0_lo, g - 3)
                w = slice(c * ROWS, (c + 1) * ROWS)
                product(BANK[2 + g % 4][:], (ff0h[:, w], ff0l[:, w]), (xth[:, xt(u)], xtl[:, xt(u)])).then_inc(h0_ps, 1)

            def down0(g):
                u, c = divmod(g, CH0)
                pe.wait_ge(h0_lo, g + 1)
                if c == 0:
                    if u >= 1:
                        pe.wait_ge(o1_sb, u)
                    else:
                        pe.wait_ge(x_new[0], UNITS)
                w = slice(DFF0 + c * D, DFF0 + (c + 1) * D)
                nc.tensor.matmul(OT[:], ff0h[:, w], acth[:, g % 3, :], start=(c == 0), stop=False)
                nc.tensor.matmul(OT[:], ff0h[:, w], actl[:, g % 3, :], start=False, stop=False)
                return nc.tensor.matmul(OT[:], ff0l[:, w], acth[:, g % 3, :], start=False, stop=(c == CH0 - 1))

            def gate_logits(u):
                if u >= 1:
                    pe.wait_ge(gate_sb, u)
                w = slice(DFF0 + CH0 * D, DFF0 + CH0 * D + EXPERTS)
                for k in range(PER_UNIT):
                    tok = slice(u * UTOK + k * ROWS, u * UTOK + (k + 1) * ROWS)
                    last = product(AUX[:, k * EXPERTS:(k + 1) * EXPERTS], (xth[:, tok], xtl[:, tok]),
                                   (ff0h[:, w], ff0l[:, w]))
                last.then_inc(gate_ps, 1)

            pe.wait_ge(g_lo[0], 2)
            pe.wait_ge(vw_sb[0], 2)
            pe.wait_ge(kv1_done, 1)
            pe.wait_ge(consts, 5)
            attention(0, up0)

            for g in range(UNITS * CH0):
                u, c = divmod(g, CH0)
                last = down0(g)
                if c == 0:
                    gate_logits(u)
                    transpose_x(UNITS + u + 1)
                if g + 3 < UNITS * CH0:
                    up0(g + 3)
                if c == CH0 - 1:
                    last.then_inc(o_ps[1], 1)
                    transpose_back(u)

            pe.wait_ge(kvb_done, 2 * UNITS)
            pe.wait_ge(h0_lo, UNITS * CH0)
            for u in range(UNITS):
                nc.tensor.matmul(BANK[2 + u][:], wq1_sb[:], KB[:, u, :], start=True, stop=True).then_inc(g_ps[1], 1)
            for u in range(UNITS):
                pe.wait_ge(g_lo[1], u + 1)
                for c in range(4):
                    last = nc.tensor.matmul(BANK[2 + u][:, c * ROWS:(c + 1) * ROWS],
                                            VB[:, u, c * ROWS:(c + 1) * ROWS], wo1_sb[:], start=True, stop=True)
                last.then_inc(vw_ps[1], 1)
            def up(u, j, parts=(0, 1)):
                e, c = divmod(j % NG, NCH)
                n = CHUNKS[c]
                tok = bass.ds((u + j // NG) * UTOK, UTOK)
                xs = (xth[:, tok], xtl[:, tok])
                first = isinstance(u, int) and u == 0
                if j == 0 and first:
                    pe.wait_ge(xt_lo, 3 * UNITS + 1)
                    pe.wait_ge(s_sb[1], TILES)
                if j == 1 and first:
                    pe.wait_ge(pt_sb[1], TILES - 1)
                if c == 0:
                    pe.wait_ge(raw_split, e + 2)
                if j == NG:
                    pe.wait_ge(xt_lo, u + (3 * UNITS + 2))
                for k, (bank, done) in enumerate(((hbank(j), h_ps), (vbank(j), v_ps))):
                    if k not in parts:
                        continue
                    if k == 0 and not (first and j < 2):
                        pe.wait_ge(act_done, u * NG + (j - 1))
                    if k == 1 and not (first and j < 1):
                        pe.wait_ge(silu_done, u * NG + j)
                    w = slice(k * HID + c * ROWS, k * HID + c * ROWS + n)
                    product(bank[0:n, :], (ewh[:, e, w], ewl[:, e, w]), xs).then_inc(done, 1)

            def down(u, j):
                e, c = divmod(j % NG, NCH)
                r, n = j % 3, CHUNKS[c]
                pe.wait_ge(act_lo, u * NG + (j + 1))
                if j == P_GL and not isinstance(u, int):
                    pe.wait_ge(glT_sb, u + 2)
                if c == 0:
                    if e == 1:
                        pe.wait_ge(shared_sb, u + (1 + j // NG))
                    elif e > 1:
                        pe.wait_ge(gated_done, u * EXPERTS + (e - 1))
                    elif j >= NG:
                        pe.wait_ge(gated_done, u * EXPERTS + EXPERTS)
                    else:
                        pe.wait_ge(x_new[2], UNITS)
                w = slice(2 * HID + c * D, 2 * HID + (c + 1) * D)
                wh, wl = ewh[0:n, e, w], ewl[0:n, e, w]
                ah, al = acth[0:n, r, :], actl[0:n, r, :]
                nc.tensor.matmul(OT[:], wh, ah, start=(c == 0), stop=False)
                nc.tensor.matmul(OT[:], wh, al, start=False, stop=False)
                last = nc.tensor.matmul(OT[:], wl, ah, start=False, stop=(c == NCH - 1))
                if c == NCH - 1:
                    last.then_inc(o_ps[3], 1)

            def experts(u, j0, j1, last_up):
                for j in range(j0, j1):
                    if j + AHEAD <= last_up:
                        up(u, j + AHEAD)
                    if j == NG + BACK_AT:
                        back(u)
                    down(u, j)
                    if not isinstance(u, int):
                        prepare(u + 1, j)
                    elif j == FIRST_WT - 1:
                        gate_weights_t(0)

            def back(u):
                pe.wait_ge(acc_done, u * EXPERTS + (EXPERTS + 2))
                pe.wait_ge(x_new[2], UNITS)
                for k in range(PER_UNIT):
                    last = nc.tensor.transpose(OB[:, k * ROWS:(k + 1) * ROWS], acc[:, k * ROWS:(k + 1) * ROWS], ident[:])
                last.then_inc(b_ps[3], 1)

            def gate_logits_t(n):
                w = slice(DFF0 + CH0 * D + EXPERTS, FF0COLS)
                xs = bass.ds(n * UTOK, UTOK)
                pe.wait_ge(xt_lo, n + (3 * UNITS + 1))
                product(AUX[:], (ff0h[:, w], ff0l[:, w]), (xth[:, xs], xtl[:, xs])).then_inc(glT_ps, 1)

            def gate_logits_back(n):
                for k in range(PER_UNIT):
                    last = nc.tensor.transpose(BANK[5][:, k * EXPERTS:(k + 1) * EXPERTS],
                                               glT[:, k * ROWS:(k + 1) * ROWS], ident[0:EXPERTS, 0:EXPERTS])
                last.then_inc(gl_ps, 1)

            def gate_weights_t(n):
                pe.wait_ge(w1_done, n + 1)
                for k in range(PER_UNIT):
                    last = nc.tensor.transpose(AUX[0:EXPERTS, k * ROWS:(k + 1) * ROWS], gw[:, k, :], ident[:])
                last.then_inc(wT_ps, 1)

            def prepare(n, j):
                if j == P_XT:
                    pe.wait_ge(xn_done, n + (3 * UNITS + 1))
                    for k in range(PER_UNIT):
                        last = nc.tensor.transpose(XT[:, k * ROWS:(k + 1) * ROWS], xn[:, 0, k, :], ident[:])
                    last.then_inc(xt_ps, 1)
                if j == P_GLT:
                    gate_logits_t(n)
                if j == P_GL:
                    gate_logits_back(n)
                if j == P_WT:
                    gate_weights_t(n)

            def begin_experts(k):
                if k == 0:
                    up(0, 0)
                if k == 1:
                    up(0, 1, (0,))

            pe.wait_ge(vw_sb[1], UNITS)
            pe.wait_ge(mask_done, 1)
            attention(1, begin_experts)
            gate_logits_t(0)
            pe.wait_ge(glT_sb, 1)
            gate_logits_back(0)
            up(0, 1, (1,))
            experts(0, 0, EDGE, EDGE - 1 + AHEAD)
            with pe.Fori(0, UNITS - 1) as u:
                experts(u, EDGE, NG + EDGE, NG + EDGE - 1 + AHEAD)
            experts(UNITS - 1, EDGE, NG, NG - 1)
            back(UNITS - 1)


def kernel(**inputs):
    import numpy as np
    import concourse.bacc as bacc
    from concourse.bass_utils import run_bass_kernel_spmd

    a = {k: np.asarray(v) for k, v in inputs.items()}

    def rows(w, n):
        out = np.zeros((n * ROWS, w.shape[1]), w.dtype)
        out[:w.shape[0]] = w
        return out.reshape(n, ROWS, w.shape[1]).transpose(1, 0, 2).reshape(ROWS, -1)

    def expert(w1, w2, w3):
        return np.concatenate([w1.T, w2.T, rows(w3.T, NCH)], axis=1)

    ew = [expert(a["L1_ffn_Ws1"], a["L1_ffn_Ws2"], a["L1_ffn_Ws3"])]
    ew += [expert(a["L1_ffn_W1"][e], a["L1_ffn_W2"][e], a["L1_ffn_W3"][e]) for e in range(EXPERTS)]
    arrays = {
        "x": a["x"].reshape(UNITS, PER_UNIT, ROWS, D).transpose(0, 2, 1, 3),
        "ctx_t": a["ctx_768"].reshape(UNITS * KEYS, CTX).T,
        "mask": a["mask_BxS2_bf1"].view(np.uint8).reshape(1, -1),
        "gx": a["g_xattn"].reshape(1, 2),
        "gf": a["g_ffn"].reshape(1, 2),
        "wk0": a["L0_xattn_Wk"],
        "wq0t": a["L0_xattn_Wq"].reshape(D, HEADS[0], 64).transpose(2, 1, 0),
        "wv0": a["L0_xattn_Wv"],
        "wo0": a["L0_xattn_Wout"].reshape(HEADS[0], 64, D).transpose(1, 0, 2),
        "bout": a["L0_xattn_bout"].reshape(1, D),
        "wk1": a["L1_xattn_Wk"],
        "wq1t": a["L1_xattn_Wq"].T,
        "wv1": a["L1_xattn_Wv"],
        "wo1": a["L1_xattn_Wo"],
        "head_mask": np.repeat(np.eye(HEADS[1], dtype=np.float32), HEAD_DIM[1], axis=0),
        "ff0": np.concatenate([a["L0_ffn_w1"], rows(a["L0_ffn_w2"], CH0), a["L0_ffn_Wg"], a["L1_ffn_Wg"].T,
                               np.zeros((D, ROWS - EXPERTS), np.float32)], axis=1),
        "ew": np.stack(ew),
        "bias1": a["L1_ffn_routing_bias"].reshape(1, EXPERTS),
        "ident_in": np.eye(ROWS, dtype=np.float32),
    }
    arrays = {k: np.ascontiguousarray(v) for k, v in arrays.items()}
    nc = bacc.Bacc("TRN2", target_bir_lowering=False, num_devices=1)
    args = {k: nc.dram_tensor(k + "_dram", v.shape, mybir.dt.from_np(v.dtype), kind="ExternalInput").ap()
            for k, v in arrays.items()}
    scratch = nc.dram_tensor("gate_scratch", (UNITS * EXPERTS, UTOK), mybir.dt.float32, kind="Internal").ap()
    out = nc.dram_tensor("out_dram", (UNITS, ROWS, PER_UNIT, D), mybir.dt.float32, kind="ExternalOutput").ap()
    flamingo_kernel(nc, **args, gate_scratch=scratch, out=out)
    r = run_bass_kernel_spmd(nc, [{k + "_dram": v for k, v in arrays.items()}], core_ids=[0])
    got = np.asarray(r.results[0]["out_dram"])
    return np.ascontiguousarray(got.transpose(0, 2, 1, 3)).reshape(UNITS, UTOK, D)
```

```python
import concourse.bass as bass
from concourse import mybir
from contextlib import ExitStack

ROWS, D = 128, 128
UNITS, TILES = 4, 16
PER_UNIT = TILES // UNITS
UTOK = ROWS * PER_UNIT
KEYS, CTX = 32, 96
HEADS = (8, 16)
HEAD_DIM = (64, 8)
DFF0 = 512
CH0 = DFF0 // ROWS
EXPERTS = 8
HID = D * 2 * 4 // 3
FULL = HID // ROWS
REST = HID - FULL * ROWS
PACK = ROWS // EXPERTS
PACKED = REST // PACK
ENDS = REST - PACKED * PACK
NG = FULL * (1 + EXPERTS) + PACKED + 1
FIRST_GATED = FULL
GATED = NG - FIRST_GATED
CCOLS = 3 * ROWS
PER_LOAD = 3
LOADS = NG // PER_LOAD
assert EXPERTS * ENDS + REST <= ROWS and NG % PER_LOAD == 0
FF0COLS = DFF0 + CH0 * D + EXPERTS + ROWS
EPS = 1e-5
F32_EPS = 1.1920928955078125e-07
LOWEST_BF16 = -3.3895313892515355e38


def flamingo_kernel(nc, x, ctx_wk0, wv0, wq0t, wo0, wkv1, square_w, small, bout, mask, ff0, ew,
                    gate_scratch, out):
    f32, f32r, bf16 = mybir.dt.float32, mybir.dt.float32r, mybir.dt.bfloat16
    ALU, ACT, AX = mybir.AluOpType, mybir.ActivationFunctionType, mybir.AxisListType

    ctx = ExitStack()
    with ctx:
        def sb(name, shape, dt=f32):
            return ctx.enter_context(nc.sbuf_tensor(name, shape, dt))

        def sem(name):
            return ctx.enter_context(nc.semaphore(name))

        X = sb("X", [ROWS, TILES, D])
        ew_raw = sb("ew_raw", [ROWS, 2, max(PER_LOAD * CCOLS, FF0COLS)])
        ewh = sb("ewh", [ROWS, NG, CCOLS], f32r)
        ewl = sb("ewl", [ROWS, NG, CCOLS], f32r)
        ff0h = sb("ff0h", [ROWS, FF0COLS], f32r)
        ff0l = sb("ff0l", [ROWS, FF0COLS], f32r)
        GH = [sb(f"g{i}_hi", [ROWS, UNITS, HEADS[i] * KEYS], f32r) for i in range(2)]
        GL = [sb(f"g{i}_lo", [ROWS, UNITS, HEADS[i] * KEYS], f32r) for i in range(2)]
        VW = [sb(f"vw{i}", [ROWS, UNITS * HEADS[i] // 4, D]) for i in range(2)]
        xth = sb("xt_hi", [ROWS, UNITS * UTOK], f32r)
        xtl = sb("xt_lo", [ROWS, UNITS * UTOK], f32r)
        acth = sb("act_hi", [ROWS, 3, UTOK], f32r)
        actl = sb("act_lo", [ROWS, 3, UTOK], f32r)
        xn = sb("xn", [ROWS, 2, PER_UNIT, D])
        oT = sb("oT", [ROWS, UTOK])
        glT = xn[0:EXPERTS, 1].rearrange("p k d -> p (k d)")
        arena = sb("arena", [ROWS, 14 * UTOK])
        SC = [arena[:, UTOK * i:UTOK * (i + 1)] for i in range(6)]
        PTS = arena[:, 6 * UTOK:14 * UTOK].rearrange("p (i c n) -> p i c n", i=2, c=4)
        wv0_sb = SC[2]
        ctx_wk0_sb = arena[:, 3 * UTOK:5 * UTOK]
        ctx_sb, wk0_sb = ctx_wk0_sb[0:CTX, 0:ROWS], ctx_wk0_sb[0:CTX, ROWS:ROWS + DFF0]
        wq0_sb, wo0_sb, kT0, vT0 = (arena[:, n * UTOK:(n + 1) * UTOK].rearrange("p (h n) -> p h n", h=4)
                                    for n in (6, 7, 8, 9))
        KB = arena[:, 0:UNITS * UTOK].rearrange("p (u n) -> p u n", u=UNITS)
        VB = VW[1][:].rearrange("p (u c) n -> p u (c n)", u=UNITS)
        PT = [PTS[:, t // 4, t % 4].rearrange("p (c n) -> p c n", c=4) for t in range(8)]
        raw = [ew_raw[:, 0], ew_raw[:, 1]] + [arena[:, 6 * UTOK + n * PER_LOAD * CCOLS:6 * UTOK + (n + 1) * PER_LOAD * CCOLS]
                                              for n in range(3)]
        RAW_OF = (0, 1, 0, 2, 3, 4, 1, 0, 2)
        silu = arena[:, 0:3 * UTOK].rearrange("p (i n) -> p i n", i=3)
        act = arena[:, 3 * UTOK:6 * UTOK].rearrange("p (i n) -> p i n", i=3)
        acc = arena[:, 6 * UTOK:7 * UTOK]
        free0 = [t for v in (GH[0][:].bitcast(f32), GL[0][:].bitcast(f32))
                 for t in (v[:, 0:2].rearrange("p b n -> p (b n)"), v[:, 2:4].rearrange("p b n -> p (b n)"))]
        free0 += [VW[0][:, 0:4].rearrange("p c n -> p (c n)"), VW[0][:, 4:8].rearrange("p c n -> p (c n)")]
        wT = free0[5][0:EXPERTS, :]
        wb = free0[0:5] + [arena[:, (7 + n) * UTOK:(8 + n) * UTOK] for n in range(EXPERTS + 2 - 5)]
        WB_PACKED, WB_LAST = EXPERTS, EXPERTS + 1
        wkv1_sb = sb("wkv1_sb", [CTX, 2, D])
        square_sb = sb("square_sb", [ROWS, 3 * D + HEADS[1]])
        ident, wq1_sb, wo1_sb = (square_sb[:, n * D:(n + 1) * D] for n in range(3))
        hm_sb = square_sb[:, 3 * D:3 * D + HEADS[1]]
        kv1 = sb("kv1", [D, 2, ROWS])
        mask_i = sb("mask_i", [1, UNITS * KEYS], mybir.dt.uint8)
        mask_b = sb("mask_b", [1, UNITS * KEYS], bf16)
        ones_b = sb("ones_b", [1, ROWS], bf16)
        small_sb = sb("small_sb", [ROWS, 4 + EXPERTS])
        gains, b1_sb = small_sb[:, 0:4], small_sb[:, 4:4 + EXPERTS]
        tg = sb("tg", [ROWS, 4])
        bo_sb = sb("bo_sb", [1, D])
        ones_f = sb("ones_f", [1, ROWS])
        stats = sb("stats", [ROWS, PER_UNIT, 6])
        mv = sb("mv", [ROWS, 2, PER_UNIT, 2])
        nmr = sb("nmr", [ROWS, 2, PER_UNIT])
        ve = sb("ve", [ROWS, 2, PER_UNIT])
        mhalf = sb("mhalf", [ROWS, PER_UNIT])
        rstd = sb("rstd", [ROWS, 2, PER_UNIT])
        smax = sb("smax", [ROWS, 6, HEADS[1]])
        ssum = sb("ssum", [ROWS, 6, HEADS[1]])
        srec = sb("srec", [ROWS, 6, HEADS[1]])
        gl = sb("gl", [ROWS, PER_UNIT, EXPERTS])
        gs = sb("gs", [ROWS, PER_UNIT, EXPERTS])
        ge = sb("ge", [ROWS, PER_UNIT, EXPERTS])
        gq = sb("gq", [ROWS, PER_UNIT, EXPERTS])
        gp = sb("gp", [ROWS, PER_UNIT, EXPERTS])
        gt = sb("gt", [ROWS, PER_UNIT, EXPERTS])
        gr = sb("gr", [ROWS, PER_UNIT, EXPERTS])
        gw = sb("gw", [ROWS, PER_UNIT, EXPERTS])
        go = sb("go", [ROWS, PER_UNIT, EXPERTS])
        g4 = sb("g4", [ROWS, 6, PER_UNIT])
        w0 = sb("w0", [ROWS, 2, PER_UNIT])

        BANK = [ctx.enter_context(nc.psum_tensor(f"bank{i}", [ROWS, 512], f32)) for i in range(8)]
        XT, AUX, OT, OB = BANK[0], BANK[1], BANK[6], BANK[7]

        in_k0, in_wq0, in_wo0, in_wv0 = sem("in_k0"), sem("in_wq0"), sem("in_wo0"), sem("in_wv0")
        in_square, in_kv1, in_small = sem("in_square"), sem("in_kv1"), sem("in_small")
        in_x = [sem(f"in_x{u}") for u in range(UNITS)]
        in_ew = [sem(f"in_ew{n}") for n in range(1 + LOADS)]
        raw_rounded, raw_split = sem("raw_rounded"), sem("raw_split")
        consts = sem("consts")
        tanh_done, mask_done = sem("tanh_done"), sem("mask_done")
        k0_ps, v0_ps, k0_sb, v0_sb = sem("k0_ps"), sem("v0_ps"), sem("k0_sb"), sem("v0_sb")
        kv1_ps, kv1_done, kvb_done = sem("kv1_ps"), sem("kv1_done"), sem("kvb_done")
        g_ps = [sem(f"g{i}_ps") for i in range(2)]
        g_hi = [sem(f"g{i}_hi_done") for i in range(2)]
        g_lo = [sem(f"g{i}_lo_done") for i in range(2)]
        vw_ps = [sem(f"vw{i}_ps") for i in range(2)]
        vw_sb = [sem(f"vw{i}_sb") for i in range(2)]
        ln_step, ln_var, ln_inv, ln_rstd, xn_done = sem("ln_step"), sem("ln_var"), sem("ln_inverse_std"), sem("ln_rstd"), sem("xn_done")
        xt_ps, xt_hi, xt_lo = sem("xt_ps"), sem("xt_hi_done"), sem("xt_lo_done")
        s_ps = [sem(f"scores{i}_ps") for i in range(2)]
        s_sb = [sem(f"scores{i}_sb") for i in range(2)]
        s_max = [sem(f"scores{i}_max") for i in range(2)]
        s_sub = [sem(f"scores{i}_shifted") for i in range(2)]
        p_exp = [sem(f"probs{i}_exp") for i in range(2)]
        p_sum = [sem(f"probs{i}_sum") for i in range(2)]
        p_rec = [sem(f"probs{i}_rec") for i in range(2)]
        p_norm = [sem(f"probs{i}_norm") for i in range(2)]
        pt_ps = [sem(f"probsT{i}_ps") for i in range(2)]
        pt_sb = [sem(f"probsT{i}_sb") for i in range(2)]
        o_ps = [sem(f"out{s}_ps") for s in range(4)]
        o1_sb = sem("out1_sb")
        b_ps = {s: sem(f"back{s}_ps") for s in (1, 3)}
        x_new = [sem(f"x_new{s}") for s in range(4)]
        h0_ps, h0_hi, h0_lo = sem("h0_ps"), sem("h0_hi"), sem("h0_lo")
        gate_ps, gate_sb, gate_step = sem("gate_ps"), sem("gate_sb"), sem("gate_step")
        glT_ps, glT_sb, gl_ps, chain = sem("glT_ps"), sem("glT_sb"), sem("gl_ps"), sem("gate_chain")
        top_sub, top_exp = sem("top_sub"), sem("top_exp")
        gate_sub, gate_exped, w1_done = sem("gate_sub"), sem("gate_exp"), sem("w1_done")
        wT_ps, wT_sb, w_out = sem("wT_ps"), sem("wT_sb"), sem("w_out")
        wb_in = [sem(f"wb_in{i}") for i in range(EXPERTS + 2)]
        h_ps, v_ps, silu_done, act_done = sem("h_ps"), sem("v_ps"), sem("silu_done"), sem("act_done")
        act_hi, act_lo = sem("act_hi_done"), sem("act_lo_done")
        act_gated, sum_sb, last_slot = sem("act_gated"), sem("sum_sb"), sem("last_slot_free")
        stored = sem("stored")

        def xt(u):
            return slice(u * UTOK, (u + 1) * UTOK)

        def heads_of(view, n):
            return view.rearrange("p (h j) -> p h j", h=n)

        LAG_EXP, LAG_SUM, LAG_NORM, LAG_PT, LAG_AV, LAG_RES = 1, 1, 2, 3, 4, 5
        STEPS = TILES + LAG_RES
        TAIL_GLT, TAIL_GLT_SB, TAIL_GL, TAIL_EXP, TAIL_WT = 15, 16, 16, 17, 18
        TAIL_GATES = {17: (0, 1, 2), 18: (3, 4, 5, 6, 7)}

        HBANK = BANK[2:5]

        def unit_ends(t):
            return 0 <= t < TILES and t % PER_UNIT == PER_UNIT - 1

        AHEAD, SUM_AT, BACK_AT, RES_AT, EDGE = 3, 2, 1, 4, 5
        UP = BANK[2:6]

        def hbank(j):
            return UP[2 * j % 4]

        def vbank(j):
            return UP[(2 * j + 1) % 4]

        def gates_of(c):
            if c < FULL * (1 + EXPERTS):
                return c // FULL - 1, ROWS
            return (WB_PACKED, ROWS) if c < NG - 1 else (WB_LAST, EXPERTS * ENDS)

        P_STATS, P_AGGR, P_VAR, P_RSTD, P_NORM, P_XT, P_HI, P_LO = 5, 6, 7, 7, 9, 8, 12, 12
        P_GLT, P_GLT_SB, P_GL, P_EXP, P_WT, P_WT_SB = 10, 14, 12, 17, 18, 22
        GATE_STEPS = (15, 16, 16, 17, 17, 18, 19, 20)
        CHAIN = 12

        block = ctx.enter_context(nc.Block())

        @block.sync
        def _(sp):
            sp.dma_start(ctx_wk0_sb[0:CTX, 0:ROWS + DFF0], ctx_wk0).then_inc(in_k0, 16)
            sp.dma_start(wq0_sb, wq0t).then_inc(in_wq0, 16)
            sp.dma_start(square_sb[:], square_w).then_inc(in_square, 16)
            sp.dma_start(wv0_sb[0:CTX, :], wv0).then_inc(in_wv0, 16)
            sp.dma_start(wo0_sb, wo0).then_inc(in_wo0, 16)
            for u in range(1, UNITS):
                sp.dma_start(X[:, u * PER_UNIT:(u + 1) * PER_UNIT, :], x[u]).then_inc(in_x[u], 16)
                if u == 1:
                    sp.dma_start(small_sb[:], small.partition_broadcast(ROWS)).then_inc(in_small, 16)
                    sp.dma_start(bo_sb[:], bout).then_inc(in_small, 16)
                    sp.dma_start(mask_i[:], mask).then_inc(in_small, 16)
            sp.dma_start(raw[0][:, 0:FF0COLS], ff0).then_inc(in_ew[0], 16)
            for n in range(1, 1 + LOADS):
                before = [m for m in range(n) if RAW_OF[m] == RAW_OF[n]]
                if before:
                    sp.wait_ge(raw_split, before[-1] + 1)
                elif RAW_OF[n] == 2:
                    sp.wait_ge(o_ps[0], TILES)
                sp.dma_start(raw[RAW_OF[n]][:, 0:PER_LOAD * CCOLS], ew[n - 1]).then_inc(in_ew[n], 16)

            def gate_weights(u):
                sp.wait_ge(wT_sb, u + 1)
                rows = slice(u * EXPERTS, (u + 1) * EXPERTS)
                sp.dma_start(gate_scratch[rows, :], wT).then_inc(w_out, 16)
                sp.wait_ge(w_out, (u + 1) * 16)
                for n in range(EXPERTS + 2):
                    if u >= 1:
                        last = max(c for c in range(FIRST_GATED, NG) if gates_of(c)[0] == n)
                        sp.wait_ge(act_gated, (u - 1) * GATED + last - FIRST_GATED + 1)
                    elif n == 5:
                        sp.wait_ge(o_ps[2], TILES)
                    if n < EXPERTS:
                        sp.dma_start(wb[n], gate_scratch[u * EXPERTS + n:u * EXPERTS + n + 1, :].partition_broadcast(ROWS)
                                     ).then_inc(wb_in[n], 16)
                    else:
                        k = PACK if n == WB_PACKED else ENDS
                        sp.dma_start(wb[n][0:EXPERTS * k, :],
                                     gate_scratch[rows, None, :].to_broadcast([EXPERTS, k, UTOK])).then_inc(wb_in[n], 16)

            for u in range(UNITS + 1):
                if u < UNITS:
                    gate_weights(u)
                if u >= 1:
                    sp.wait_ge(x_new[3], u)
                    sp.dma_start(out[u - 1], X[:, (u - 1) * PER_UNIT:u * PER_UNIT, :]).then_inc(stored, 16)
            sp.wait_ge(stored, 16 * UNITS)

        @block.gpsimd
        def _(pool):
            nc.gpsimd.memset(mhalf[:], -0.5).then_inc(consts, 1)
            nc.gpsimd.memset(ones_b[:], 1.0).then_inc(consts, 1)
            nc.gpsimd.memset(ones_f[:], 1.0).then_inc(consts, 1)
            nc.gpsimd.memset(go[:], 1.0).then_inc(consts, 1)
            pool.wait_ge(consts, 4)
            nc.gpsimd.memset(go[:, :, 0:1], 0.0).then_inc(consts, 1)

            def inverse_std(q):
                pool.wait_ge(ln_var, q + 1)
                nc.gpsimd.tensor_tensor(rstd[:, q % 2, :], ve[:, q % 2, :], mhalf[:], ALU.pow).then_inc(ln_inv, 1)

            def split_low_0(part):
                w = slice(part * (FF0COLS // 4), (part + 1) * (FF0COLS // 4))
                if part == 0:
                    pool.wait_ge(raw_rounded, 1)
                last = nc.gpsimd.tensor_tensor(ff0l[:, w], raw[0][:, w], ff0h[:, w].bitcast(f32), ALU.subtract)
                if part == 3:
                    last.then_inc(raw_split, 1)

            def split_low(n):
                pool.wait_ge(raw_rounded, n + 1)
                c = slice((n - 1) * PER_LOAD, n * PER_LOAD)
                nc.gpsimd.tensor_tensor(ewl[:, c, :],
                                        raw[RAW_OF[n]][:, 0:PER_LOAD * CCOLS].rearrange("p (c n) -> p c n", c=PER_LOAD),
                                        ewh[:, c, :].bitcast(f32), ALU.subtract).then_inc(raw_split, 1)

            def attention(i):
                nh = HEADS[i]
                for s in range(TILES + LAG_NORM):
                    t = s - LAG_NORM
                    if t >= 0:
                        pool.wait_ge(p_rec[i], t + 1)
                        v = heads_of(SC[t % 6][:, 0:nh * KEYS], nh)
                        nc.gpsimd.tensor_tensor(v, v, srec[:, t % 6, 0:nh, None].to_broadcast([ROWS, nh, KEYS]),
                                                ALU.mult).then_inc(p_norm[i], 1)
                    if s < TILES:
                        pool.wait_ge(s_max[i], s + 1)
                        v = heads_of(SC[s % 6][:, 0:nh * KEYS], nh)
                        nc.gpsimd.tensor_tensor(v, v, smax[:, s % 6, 0:nh, None].to_broadcast([ROWS, nh, KEYS]),
                                                ALU.subtract).then_inc(s_sub[i], 1)
                        if s % PER_UNIT == 1 and 2 * i * UNITS + s // PER_UNIT + 2 <= 3 * UNITS:
                            inverse_std(2 * i * UNITS + s // PER_UNIT + 2)
                    if i == 0 and s in (6, 8, 10, 12):
                        split_low_0(s // 2 - 3)

            def spread(dst, n, u):
                nc.gpsimd.tensor_tensor(
                    heads_of(dst[:, u, :], HEADS[1]),
                    kv1[:, n, None, u * KEYS:(u + 1) * KEYS].to_broadcast([D, HEADS[1], KEYS]),
                    hm_sb[:, :, None].to_broadcast([D, HEADS[1], KEYS]), ALU.mult).then_inc(kvb_done, 1)

            inverse_std(0)
            inverse_std(1)
            attention(0)
            pool.wait_ge(kv1_done, 1)
            pool.wait_ge(in_square, 16)
            pool.wait_ge(pt_ps[0], TILES)
            for u in range(UNITS):
                spread(KB, 0, u)
                inverse_std(UNITS + u + 2)
                spread(VB, 1, u)
                split_low(1 + 2 * u)
                split_low(2 + 2 * u)
            attention(1)

            def experts(u, j0, j1):
                for j in range(j0, j1):
                    c, r = j % NG, j % 3
                    if c >= FIRST_GATED:
                        n, rows = gates_of(c)
                        pool.wait_ge(act_done, u * NG + (j + 1))
                        if c == FIRST_GATED or gates_of(c - 1)[0] != n:
                            pool.wait_ge(wb_in[n], u * 16 + (j // NG + 1) * 16)
                        nc.gpsimd.tensor_tensor(act[0:rows, r, :], act[0:rows, r, :], wb[n][0:rows, :],
                                                ALU.mult).then_inc(act_gated, 1)
                    if j == P_RSTD and not isinstance(u, int):
                        pool.wait_ge(ln_var, u + (3 * UNITS + 2))
                        nc.gpsimd.tensor_tensor(rstd[:, 0, :], ve[:, 0, :], mhalf[:], ALU.pow).then_inc(ln_rstd, 1)

            experts(0, 0, EDGE)
            with pool.Fori(0, UNITS - 1) as u:
                experts(u, EDGE, NG + EDGE)
            experts(UNITS - 1, EDGE, NG)

        @block.scalar
        def _(act_e):
            act_e.dma_start(X[:, 0:PER_UNIT, :], x[0]).then_inc(in_x[0], 16)
            act_e.dma_start(wkv1_sb[:], wkv1).then_inc(in_kv1, 16)

            def round_high(n):
                act_e.wait_ge(in_ew[n], 16)
                if n == 0:
                    nc.scalar.activation(ff0h[:], raw[0][:, 0:FF0COLS], ACT.Copy).then_inc(raw_rounded, 1)
                else:
                    nc.scalar.activation(ewh[:, (n - 1) * PER_LOAD:n * PER_LOAD, :],
                                         raw[RAW_OF[n]][:, 0:PER_LOAD * CCOLS].rearrange("p (c n) -> p c n", c=PER_LOAD),
                                         ACT.Copy).then_inc(raw_rounded, 1)

            def normalise(q, tiles=range(PER_UNIT)):
                act_e.wait_ge(ln_rstd, q + 1)
                if q >= 2:
                    act_e.wait_ge(xt_ps, q - 1)
                for k in tiles:
                    last = nc.scalar.activation(xn[:, q % 2, k, :], X[:, q % UNITS * PER_UNIT + k, :], ACT.Identity,
                                                scale=rstd[:, q % 2, k:k + 1], bias=nmr[:, q % 2, k:k + 1])
                if k == PER_UNIT - 1:
                    last.then_inc(xn_done, 1)

            def transposed_high(q):
                act_e.wait_ge(xt_ps, q + 1)
                nc.scalar.activation(xth[:, xt(q % UNITS)], XT[:], ACT.Copy).then_inc(xt_hi, 1)

            def gate_weights_out(n):
                act_e.wait_ge(wT_ps, n + 1)
                if not isinstance(n, int):
                    act_e.wait_ge(w_out, n * 16)
                nc.scalar.activation(wT, AUX[0:EXPERTS, :], ACT.Copy).then_inc(wT_sb, 1)

            def gate_exp(n):
                act_e.wait_ge(top_sub, n + 1)
                nc.scalar.activation(ge[:], gq[:], ACT.Exp).then_inc(top_exp, 1)

            def gate_logits_out(n):
                act_e.wait_ge(glT_ps, n + 1)
                nc.scalar.activation(glT, AUX[0:EXPERTS, :], ACT.Copy).then_inc(glT_sb, 1)

            def attention(i):
                nh = HEADS[i]
                nch = nh // 4
                scale = float(HEAD_DIM[i]) ** -0.5
                for s in range(TILES + LAG_PT):
                    if s < TILES:
                        act_e.wait_ge(s_ps[i], s + 1)
                        if s >= 6:
                            act_e.wait_ge(pt_ps[i], s - 5)
                        nc.scalar.activation(SC[s % 6][:, 0:nh * KEYS], BANK[2 + s % 2][:, 0:nh * KEYS],
                                             ACT.Copy).then_inc(s_sb[i], 1)
                        if s == 2 if i == 0 and s < PER_UNIT else s % PER_UNIT == 1:
                            transposed_high(2 * i * UNITS + s // PER_UNIT + 1)
                    if i == 1 and s < 3:
                        ffn_tail(UNITS - 1, s)
                    t = s - LAG_EXP
                    if 0 <= t < TILES:
                        act_e.wait_ge(s_sub[i], t + 1)
                        nc.scalar.activation(SC[t % 6][:, 0:nh * KEYS], SC[t % 6][:, 0:nh * KEYS], ACT.Exp,
                                             scale=scale).then_inc(p_exp[i], 1)
                    if i == 1 and s == TILES + LAG_PT - 1:
                        silu_of(0, 0)
                    t = s - LAG_PT
                    if t >= 0:
                        act_e.wait_ge(pt_ps[i], t + 1)
                        if t >= 8:
                            act_e.wait_ge(o_ps[2 * i], t - 7)
                        nc.scalar.activation(PT[t % 8][:, 0:nch, :],
                                             BANK[4 + t % 2][:, 0:nch * ROWS].rearrange("p (c n) -> p c n", c=nch),
                                             ACT.Copy).then_inc(pt_sb[i], 1)
                    q = 2 * i * UNITS + s // PER_UNIT + 2
                    if s < TILES and s % PER_UNIT in (2, 3) and q <= 3 * UNITS:
                        normalise(q, (0, 1) if s % PER_UNIT == 2 else (2, 3))
                    if i == 0:
                        if s == 0:
                            normalise(1)
                        if s in (2, 3):
                            vw0_out(s - 2)
                        if s == 4:
                            act_e.wait_ge(in_small, 48)
                            nc.scalar.activation(tg[:], gains, ACT.Tanh).then_inc(tanh_done, 1)
                        if s in (5, TILES + 1):
                            round_high(s // TILES)
                    if i == 1 and s == TAIL_GLT_SB:
                        gate_logits_out(0)
                    if i == 1 and s == TAIL_EXP:
                        gate_exp(0)

            def silu_of(u, j):
                act_e.wait_ge(h_ps, u * NG + (j + 1))
                nc.scalar.activation(silu[:, j % 3, :], hbank(j)[:], ACT.Silu).then_inc(silu_done, 1)

            def vw0_out(half):
                act_e.wait_ge(vw_ps[0], half + 1)
                nc.scalar.activation(VW[0][:, 4 * half:4 * half + 4, :],
                                     (AUX, BANK[5])[half][:].rearrange("p (c n) -> p c n", c=4),
                                     ACT.Copy).then_inc(vw_sb[0], 1)

            def ffn_tail(u, part):
                if part == 0:
                    act_e.wait_ge(g_ps[1], u + 1)
                    nc.scalar.activation(GH[1][:, u, :], BANK[5][:], ACT.Copy).then_inc(g_hi[1], 1)
                if part == 2:
                    act_e.wait_ge(vw_ps[1], u + 1)
                    nc.scalar.activation(VW[1][:, 4 * u:4 * u + 4, :], BANK[5][:].rearrange("p (c n) -> p c n", c=4),
                                         ACT.Copy).then_inc(vw_sb[1], 1)
                if part == 1:
                    act_e.wait_ge(o_ps[1], u + 1)
                    if u >= 1:
                        act_e.wait_ge(b_ps[1], u)
                    nc.scalar.activation(oT[:], OT[:], ACT.Copy).then_inc(o1_sb, 1)

            act_e.wait_ge(k0_ps, 1)
            nc.scalar.activation(kT0, BANK[2][:].rearrange("p (h n) -> p h n", h=4), ACT.Copy).then_inc(k0_sb, 1)
            act_e.wait_ge(kv1_ps, 1)
            nc.scalar.activation(kv1[:], BANK[3][:, 0:2 * ROWS].rearrange("p (i n) -> p i n", i=2),
                                 ACT.Copy).then_inc(kv1_done, 1)
            normalise(0)
            act_e.wait_ge(g_ps[0], 1)
            for n in range(2):
                nc.scalar.activation(
                    GH[0][:].rearrange("p b (h i j) -> p b h i j", h=4, i=2)[:, :, :, n, :],
                    BANK[6 + n][:].rearrange("p (h b j) -> p b h j", h=4, b=UNITS), ACT.Copy).then_inc(g_hi[0], 1)
            transposed_high(0)
            attention(0)

            for u in range(UNITS):
                for c in range(CH0):
                    g = u * CH0 + c
                    act_e.wait_ge(h0_ps, g + 1)
                    nc.scalar.activation(acth[:, g % 3, :], HBANK[g % 3][:], ACT.Relu).then_inc(h0_hi, 1)
                    if c < 3 and u:
                        ffn_tail(u - 1, c)
                    if c == 2:
                        transposed_high(UNITS + u + 1)
                    if c in (0, 3) and u * 2 + 2 + c // 3 <= LOADS:
                        round_high(u * 2 + 2 + c // 3)
                act_e.wait_ge(gate_sub, u + 1)
                nc.scalar.activation(ge[:], gq[:], ACT.Exp).then_inc(gate_exped, 1)
                normalise(UNITS + u + 2)
            attention(1)

            gate_weights_out(0)

            def high(u, j):
                if j % NG < FIRST_GATED:
                    act_e.wait_ge(act_done, u * NG + (j + 1))
                else:
                    act_e.wait_ge(act_gated, u * GATED + (j // NG * GATED + j % NG - FIRST_GATED + 1))
                nc.scalar.activation(acth[:, j % 3, :], act[:, j % 3, :], ACT.Copy).then_inc(act_hi, 1)

            def sum_out(u):
                act_e.wait_ge(o_ps[3], u + 1)
                nc.scalar.activation(acc, OT[:], ACT.Copy).then_inc(sum_sb, 1)

            def experts(u, j0, j1):
                for j in range(j0, j1):
                    if j >= 1:
                        silu_of(u, j)
                    if j == NG + SUM_AT:
                        sum_out(u)
                    if j >= 1:
                        high(u, j - 1)
                    if not isinstance(u, int):
                        if j == P_HI:
                            act_e.wait_ge(xt_ps, u + (3 * UNITS + 2))
                            nc.scalar.activation(xth[:, bass.ds((u + 1) * UTOK, UTOK)], XT[:], ACT.Copy
                                                 ).then_inc(xt_hi, 1)
                        if j == P_GLT_SB:
                            gate_logits_out(u + 1)
                        if j == P_EXP:
                            gate_exp(u + 1)
                        if j == P_WT_SB:
                            gate_weights_out(u + 1)

            experts(0, 0, EDGE)
            with act_e.Fori(0, UNITS - 1) as u:
                experts(u, EDGE, NG + EDGE)
            experts(UNITS - 1, EDGE, NG)
            act_e.wait_ge(last_slot, 1)
            high(UNITS - 1, NG - 1)
            sum_out(UNITS - 1)

        @block.vector
        def _(dve):
            count = [0]

            def link(ins):
                count[0] += 1
                ins.then_inc(gate_step, 1)
                dve.wait_ge(gate_step, count[0])

            def norm_stats(q):
                s, u = divmod(q, UNITS)
                if s == 0:
                    dve.wait_ge(in_x[u], 16)
                else:
                    dve.wait_ge(x_new[s - 1], u + 1)
                if q >= 2:
                    dve.wait_ge(xn_done, q - 1)
                for k in range(PER_UNIT):
                    last = nc.vector.bn_stats(stats[:, k, :], X[:, u * PER_UNIT + k, :])
                last.then_inc(ln_step, 1)

            def norm_aggregate(q):
                dve.wait_ge(ln_step, 2 * q + 1)
                for k in range(PER_UNIT):
                    last = nc.vector.bn_aggr(mv[:, q % 2, k, :], stats[:, k, :])
                last.then_inc(ln_step, 1)

            def norm_variance(q):
                dve.wait_ge(ln_step, 2 * q + 2)
                nc.vector.tensor_scalar(ve[:, q % 2, :], mv[:, q % 2, :, 1], EPS, None, ALU.add).then_inc(ln_var, 1)

            def norm_scale(q):
                dve.wait_ge(ln_inv, q + 1)
                nc.vector.scalar_tensor_tensor(nmr[:, q % 2, :], mv[:, q % 2, :, 0], -1.0, rstd[:, q % 2, :],
                                               ALU.mult, ALU.mult).then_inc(ln_rstd, 1)

            def spread(col, n=EXPERTS):
                return col.to_broadcast([ROWS, PER_UNIT, n])

            def top_two(u, part):
                if part == 0:
                    dve.wait_ge(gate_ps, u + 1)
                    nc.vector.tensor_copy(gl[:], AUX[:, 0:PER_UNIT * EXPERTS].rearrange("p (k e) -> p k e", k=PER_UNIT)
                                          ).then_inc(gate_sb, 1)
                    dve.wait_ge(gate_sb, u + 1)
                    for k in range(PER_UNIT):
                        last = nc.vector.max(gs[:, k, :], gl[:, k, :])
                    link(last)
                    nc.vector.tensor_tensor(gq[:], gs[:], spread(gs[:, :, 0:1]), ALU.subtract).then_inc(gate_sub, 1)
                if part == 1:
                    dve.wait_ge(gate_exped, u + 1)
                    nc.vector.reduce_sum(g4[:, 1, :], ge[:, :, 0:2], AX.X)
                    link(nc.vector.reduce_sum(g4[:, 0, :], ge[:], AX.X))
                    link(nc.vector.reciprocal(g4[:, 2, :], g4[:, 0, :]))
                if part == 2:
                    link(nc.vector.tensor_tensor(g4[:, 3, :], g4[:, 1, :], g4[:, 2, :], ALU.mult))
                    link(nc.vector.tensor_scalar(g4[:, 4, :], g4[:, 3, :], F32_EPS, None, ALU.max))
                if part == 3:
                    link(nc.vector.reciprocal(g4[:, 5, :], g4[:, 4, :]))
                    link(nc.vector.scalar_tensor_tensor(w0[:, u % 2, :], g4[:, 3, :], tg[:, 2:3], g4[:, 5, :],
                                                        ALU.mult, ALU.mult))

            def weighted_residual(u):
                dve.wait_ge(b_ps[1], u + 1)
                for k in range(PER_UNIT):
                    xk = X[:, u * PER_UNIT + k, :]
                    last = nc.vector.scalar_tensor_tensor(xk, OB[:, k * ROWS:(k + 1) * ROWS], w0[:, u % 2, k:k + 1],
                                                          xk, ALU.mult, ALU.add)
                last.then_inc(x_new[1], 1)

            def ffn_tail(u, c):
                if c == 0:
                    dve.wait_ge(g_hi[1], u + 1)
                    nc.vector.tensor_tensor(GL[1][:, u, :], BANK[5][:], GH[1][:, u, :].bitcast(f32),
                                            ALU.subtract).then_inc(g_lo[1], 1)
                top_two(u, 1 + c)
                if c == 2:
                    weighted_residual(u)

            def transposed_low(q):
                dve.wait_ge(xt_hi, q + 1)
                nc.vector.tensor_tensor(xtl[:, xt(q % UNITS)], XT[:], xth[:, xt(q % UNITS)].bitcast(f32),
                                        ALU.subtract).then_inc(xt_lo, 1)

            def attention(i):
                nh = HEADS[i]
                for s in range(STEPS):
                    q = 2 * i * UNITS + s // PER_UNIT + 1
                    norm_here = s < TILES and s % PER_UNIT == 1 and q + 1 <= 3 * UNITS
                    if s < TILES:
                        dve.wait_ge(s_sb[i], s + 1)
                        if i == 1 and s < 6:
                            dve.wait_ge(p_norm[0], TILES)
                        nc.vector.reduce_max(smax[:, s % 6, 0:nh], heads_of(SC[s % 6][:, 0:nh * KEYS], nh),
                                             AX.X).then_inc(s_max[i], 1)
                    if norm_here:
                        norm_aggregate(q + 1)
                    if s < TILES and s % PER_UNIT == 2 and q + 1 <= 3 * UNITS:
                        norm_scale(q + 1)
                    t = s - LAG_SUM
                    if 0 <= t < TILES:
                        dve.wait_ge(p_exp[i], t + 1)
                        nc.vector.reduce_sum(ssum[:, t % 6, 0:nh], heads_of(SC[t % 6][:, 0:nh * KEYS], nh),
                                             AX.X).then_inc(p_sum[i], 1)
                    if norm_here:
                        norm_variance(q + 1)
                    if 0 <= t < TILES:
                        dve.wait_ge(p_sum[i], t + 1)
                        nc.vector.reciprocal(srec[:, t % 6, 0:nh], ssum[:, t % 6, 0:nh]).then_inc(p_rec[i], 1)
                    if s < TILES and s % PER_UNIT == 2:
                        transposed_low(q)
                    if i == 1 and s < 3:
                        ffn_tail(UNITS - 1, s)
                    if i == 1 and s == STEPS - 1:
                        dve.wait_ge(pt_ps[1], TILES)
                        activation(0, 0)
                    t = s - LAG_RES
                    if unit_ends(t):
                        residual(2 * i, t // PER_UNIT)
                    if s < TILES and s % PER_UNIT == 0 and q + 1 <= 3 * UNITS:
                        norm_stats(q + 1)
                    if i == 1:
                        for part in TAIL_GATES.get(s, ()):
                            top_four(0, part)

            def top_four(n, part):
                def linked(ins, at):
                    ins.then_inc(chain, 1)
                    dve.wait_ge(chain, n * CHAIN + at)

                if part == 0:
                    dve.wait_ge(gl_ps, n + 1)
                    v = XT[:, 0:PER_UNIT * EXPERTS].rearrange("p (k e) -> p k e", k=PER_UNIT)
                    linked(nc.vector.tensor_tensor(gl[:], v, b1_sb[:, None, :].to_broadcast([ROWS, PER_UNIT, EXPERTS]),
                                                   ALU.add), 1)
                if part == 1:
                    for k in range(PER_UNIT):
                        last = nc.vector.max(gs[:, k, :], gl[:, k, :])
                    linked(last, 2)
                if part == 2:
                    linked(nc.vector.tensor_tensor(gq[:], gl[:], spread(gs[:, :, 0:1]), ALU.subtract), 3)
                    nc.vector.tensor_tensor(gt[:], gl[:], spread(gs[:, :, 3:4]), ALU.is_gt).then_inc(top_sub, 1)
                    dve.wait_ge(top_sub, n + 1)
                if part == 3:
                    linked(nc.vector.tensor_tensor(gp[:], gl[:], spread(gs[:, :, 3:4]), ALU.is_equal), 4)
                    linked(nc.vector.reduce_sum(g4[:, 0, :], gt[:], AX.X), 5)
                if part == 4:
                    linked(nc.vector.tensor_tensor_scan(gr[:].rearrange("p k e -> p (k e)"),
                                                        go[:].rearrange("p k e -> p (k e)"),
                                                        gp[:].rearrange("p k e -> p (k e)"), 0.0, ALU.mult, ALU.add), 6)
                    linked(nc.vector.tensor_tensor(gr[:], gr[:], spread(g4[:, 0, :, None]), ALU.add), 7)
                if part == 5:
                    linked(nc.vector.scalar_tensor_tensor(gr[:], gr[:], 4.0, gp[:], ALU.is_le, ALU.mult), 8)
                    linked(nc.vector.tensor_tensor(gt[:], gt[:], gr[:], ALU.add), 9)
                if part == 6:
                    dve.wait_ge(top_exp, n + 1)
                    linked(nc.vector.tensor_tensor(gp[:], ge[:], gt[:], ALU.mult), 10)
                    linked(nc.vector.reduce_sum(g4[:, 1, :], gp[:], AX.X), 11)
                if part == 7:
                    linked(nc.vector.reciprocal(g4[:, 2, :], g4[:, 1, :]), 12)
                    if not isinstance(n, int):
                        dve.wait_ge(wT_ps, n)
                    nc.vector.tensor_tensor(gw[:], gp[:], spread(g4[:, 2, :, None]), ALU.mult).then_inc(w1_done, 1)

            def residual(s, u):
                xu = X[:, u * PER_UNIT:(u + 1) * PER_UNIT, :]
                dve.wait_ge(o_ps[s], (u + 1) * PER_UNIT)
                dve.wait_ge(tanh_done, 1)
                nc.vector.scalar_tensor_tensor(xu, BANK[6 + u % 2][:].rearrange("p (k d) -> p k d", k=PER_UNIT),
                                               tg[:, s // 2:s // 2 + 1], xu, ALU.mult, ALU.add).then_inc(x_new[s], 1)

            def activation(u, j):
                dve.wait_ge(v_ps, u * NG + (j + 1))
                dve.wait_ge(silu_done, u * NG + (j + 1))
                nc.vector.tensor_tensor(act[:, j % 3, :], silu[:, j % 3, :], vbank(j)[:],
                                        ALU.mult).then_inc(act_done, 1)

            for q in (0, 1):
                norm_stats(q)
                norm_aggregate(q)
                norm_variance(q)
            norm_scale(0)
            norm_scale(1)
            for n in range(2):
                dve.wait_ge(g_hi[0], n + 1)
                v = GL[0][:].rearrange("p b (h i j) -> p b h i j", h=4, i=2)[:, :, :, n, :]
                w = GH[0][:].bitcast(f32).rearrange("p b (h i j) -> p b h i j", h=4, i=2)[:, :, :, n, :]
                nc.vector.tensor_tensor(v, BANK[6 + n][:].rearrange("p (h b j) -> p b h j", h=4, b=UNITS), w,
                                        ALU.subtract).then_inc(g_lo[0], 1)
            transposed_low(0)
            dve.wait_ge(v0_ps, 1)
            nc.vector.tensor_copy(vT0, BANK[4][:].rearrange("p (h n) -> p h n", h=4)).then_inc(v0_sb, 1)
            attention(0)

            dve.wait_ge(in_small, 48)
            nc.vector.tensor_scalar(mask_b[:], mask_i[:], 1.0, -LOWEST_BF16, ALU.subtract,
                                    ALU.mult).then_inc(mask_done, 1)
            norm_stats(UNITS + 2)
            for u in range(UNITS):
                for c in range(CH0):
                    g = u * CH0 + c
                    dve.wait_ge(h0_hi, g + 1)
                    nc.vector.scalar_tensor_tensor(actl[:, g % 3, :], HBANK[g % 3][:], 0.0,
                                                   acth[:, g % 3, :].bitcast(f32), ALU.max,
                                                   ALU.subtract).then_inc(h0_lo, 1)
                    if c == 0:
                        norm_aggregate(UNITS + u + 2)
                    if c < 3 and u:
                        ffn_tail(u - 1, c)
                    if c == 0:
                        norm_variance(UNITS + u + 2)
                    if c == 1:
                        norm_scale(UNITS + u + 2)
                    if c == 2:
                        transposed_low(UNITS + u + 1)
                        top_two(u, 0)
                    if c == CH0 - 1 and u < UNITS - 1:
                        norm_stats(UNITS + u + 3)
            attention(1)

            def prepare(n, j):
                if j == P_STATS:
                    dve.wait_ge(x_new[2], UNITS)
                    for k in range(PER_UNIT):
                        last = nc.vector.bn_stats(stats[:, k, :], X[:, bass.ds(n * PER_UNIT + k, 1), :])
                    last.then_inc(ln_step, 1)
                if j == P_AGGR:
                    for k in range(PER_UNIT):
                        last = nc.vector.bn_aggr(mv[:, 0, k, :], stats[:, k, :])
                    last.then_inc(ln_step, 1)
                if j == P_VAR:
                    dve.wait_ge(ln_step, n * 2 + (6 * UNITS + 2))
                    nc.vector.tensor_scalar(ve[:, 0, :], mv[:, 0, :, 1], EPS, None, ALU.add).then_inc(ln_var, 1)
                if j in (P_NORM, P_NORM + 1):
                    dve.wait_ge(ln_rstd, n + (3 * UNITS + 1))
                    for k in (0, 1) if j == P_NORM else (2, 3):
                        last = nc.vector.tensor_scalar(xn[:, 0, k, :], X[:, bass.ds(n * PER_UNIT + k, 1), :],
                                                       mv[:, 0, k, 0:1], rstd[:, 0, k:k + 1],
                                                       ALU.subtract, ALU.mult)
                    if j == P_NORM + 1:
                        last.then_inc(xn_done, 1)
                if j == P_LO:
                    dve.wait_ge(xt_hi, n + (3 * UNITS + 1))
                    xs = bass.ds(n * UTOK, UTOK)
                    nc.vector.tensor_tensor(xtl[:, xs], XT[:], xth[:, xs].bitcast(f32), ALU.subtract).then_inc(xt_lo, 1)
                for part, at in enumerate(GATE_STEPS):
                    if j == at:
                        top_four(n, part)

            def expert_residual(u):
                dve.wait_ge(b_ps[3], u + 1)
                xu = X[:, bass.ds(u * PER_UNIT, PER_UNIT), :]
                nc.vector.scalar_tensor_tensor(xu, OB[:].rearrange("p (k d) -> p k d", k=PER_UNIT), tg[:, 3:4], xu,
                                               ALU.mult, ALU.add).then_inc(x_new[3], 1)

            def experts(u, j0, j1):
                for j in range(j0, j1):
                    if j >= 3:
                        dve.wait_ge(act_lo, u * NG + (j - 2))
                    if j == P_AGGR and not isinstance(u, int):
                        dve.wait_ge(ln_step, u * 2 + (6 * UNITS + 3))
                    if j >= 1:
                        activation(u, j)
                    if j == NG + RES_AT:
                        expert_residual(u)
                    if not isinstance(u, int):
                        prepare(u + 1, j)
                    if j >= 1:
                        low(u, j - 1)

            def low(u, j):
                dve.wait_ge(act_hi, u * NG + (j + 1))
                nc.vector.tensor_tensor(actl[:, j % 3, :], act[:, j % 3, :], acth[:, j % 3, :].bitcast(f32),
                                        ALU.subtract).then_inc(act_lo, 1)

            experts(0, 0, EDGE)
            with dve.Fori(0, UNITS - 1) as u:
                experts(u, EDGE, NG + EDGE)
            experts(UNITS - 1, EDGE, NG)
            low(UNITS - 1, NG - 1)
            expert_residual(UNITS - 1)

        @block.tensor
        def _(pe):
            def product(out_, hi_lo, moving):
                (h, l), (mh, ml) = hi_lo, moving
                nc.tensor.matmul(out_, h, mh, start=True, stop=False)
                nc.tensor.matmul(out_, h, ml, start=False, stop=False)
                return nc.tensor.matmul(out_, l, mh, start=False, stop=True)

            def transpose_x(q):
                pe.wait_ge(xn_done, q + 1)
                if q >= 1:
                    pe.wait_ge(xt_lo, q)
                for k in range(PER_UNIT):
                    last = nc.tensor.transpose(XT[:, k * ROWS:(k + 1) * ROWS], xn[:, q % 2, k, :], ident)
                last.then_inc(xt_ps, 1)

            def transpose_back(u):
                pe.wait_ge(o1_sb, u + 1)
                if u >= 1:
                    pe.wait_ge(x_new[1], u)
                else:
                    pe.wait_ge(x_new[0], UNITS)
                for k in range(PER_UNIT):
                    last = nc.tensor.transpose(OB[:, k * ROWS:(k + 1) * ROWS], oT[:, k * ROWS:(k + 1) * ROWS],
                                               ident)
                last.then_inc(b_ps[1], 1)

            def attention(i, begin_next):
                nh = HEADS[i]
                nch, cols = nh // 4, nh * KEYS
                for s in range(TILES + LAG_AV):
                    if s < TILES:
                        u = s // PER_UNIT
                        if s % PER_UNIT == 0:
                            pe.wait_ge(xt_lo, 2 * i * UNITS + u + 1)
                            if i == 1:
                                pe.wait_ge(g_lo[1], u + 1)
                        if s >= 2:
                            pe.wait_ge(s_sb[i], s - 1)
                        tok = slice(s * ROWS, (s + 1) * ROWS)
                        bank = BANK[2 + s % 2][:, 0:cols]
                        nc.tensor.matmul(bank, xth[:, tok], GH[i][:, u, :], start=True, stop=False)
                        nc.tensor.matmul(bank, xth[:, tok], GL[i][:, u, :], start=False, stop=False)
                        last = nc.tensor.matmul(bank, xtl[:, tok], GH[i][:, u, :], start=False, stop=(i == 0))
                        if i == 1:
                            last = nc.tensor.matmul(
                                bank, ones_b[:],
                                mask_b[:, u * KEYS:(u + 1) * KEYS].rearrange("p (h j) -> p h j", h=1).to_broadcast([1, nh, KEYS]),
                                start=False, stop=True)
                        last.then_inc(s_ps[i], 1)
                    t = s - LAG_PT
                    if t in (0, 1):
                        pe.wait_ge(vw_sb[i], t + 1 if i == 0 else UNITS)
                    if 0 <= t < TILES:
                        pe.wait_ge(p_norm[i], t + 1)
                        if t >= 2:
                            pe.wait_ge(pt_sb[i], t - 1)
                        for c in range(nch):
                            last = nc.tensor.transpose(BANK[4 + t % 2][:, c * ROWS:(c + 1) * ROWS],
                                                       SC[t % 6][:, c * ROWS:(c + 1) * ROWS], ident)
                        last.then_inc(pt_ps[i], 1)
                    t = s - LAG_AV
                    if 0 <= t < TILES:
                        u, k = divmod(t, PER_UNIT)
                        pe.wait_ge(pt_sb[i], t + 1)
                        if k == 0 and u >= 2:
                            pe.wait_ge(x_new[2 * i], u - 1)
                        elif t == 0 and i == 1:
                            pe.wait_ge(x_new[1], UNITS)
                        o = BANK[6 + u % 2][:, k * ROWS:(k + 1) * ROWS]
                        if i == 0:
                            nc.tensor.matmul(o, ones_f[:], bo_sb[:], start=True, stop=False)
                        for c in range(nch):
                            last = nc.tensor.matmul(o, PT[t % 8][:, c, :], VW[i][:, u * nch + c, :],
                                                    start=(i == 1 and c == 0), stop=(c == nch - 1))
                        last.then_inc(o_ps[2 * i], 1)
                    begin_next(s)
                    if s < TILES and (s == 1 if i == 0 and s < PER_UNIT else s % PER_UNIT == 0):
                        transpose_x(2 * i * UNITS + s // PER_UNIT + 1)

            def make_kv0(w, bank, done):
                for h in range(4):
                    last = nc.tensor.matmul(bank[:, h * ROWS:(h + 1) * ROWS], w[0:CTX, h * ROWS:(h + 1) * ROWS],
                                            ctx_sb, start=True, stop=True)
                last.then_inc(done, 1)

            pe.wait_ge(in_k0, 16)
            make_kv0(wk0_sb, BANK[2], k0_ps)
            pe.wait_ge(in_kv1, 16)
            for n in range(2):
                last = nc.tensor.matmul(BANK[3][:, n * ROWS:(n + 1) * ROWS], wkv1_sb[:, n, :], ctx_sb, start=True,
                                        stop=True)
            last.then_inc(kv1_ps, 1)
            pe.wait_ge(in_wq0, 16)
            pe.wait_ge(k0_sb, 1)
            for h in range(HEADS[0]):
                rows = slice(h % 2 * 64, h % 2 * 64 + 64)
                last = nc.tensor.matmul(BANK[6 + h % 2][:, (h // 2) * ROWS:(h // 2 + 1) * ROWS],
                                        wq0_sb[rows, h // 2, :], kT0[rows, h // 2, :], start=True, stop=True)
            last.then_inc(g_ps[0], 1)
            pe.wait_ge(in_square, 16)
            transpose_x(0)
            pe.wait_ge(in_wv0, 16)
            make_kv0(wv0_sb, BANK[4], v0_ps)

            def make_vw0(half):
                pe.wait_ge(in_wo0, 16)
                pe.wait_ge(v0_sb, 1)
                for u in (2 * half, 2 * half + 1):
                    for h in range(HEADS[0]):
                        n, k = u % 2 * 2 + h // 4, h % 4
                        rows = slice(h % 2 * 64, h % 2 * 64 + 64)
                        bank = (AUX, BANK[5])[u // 2]
                        last = nc.tensor.matmul(bank[k * KEYS:(k + 1) * KEYS, n * ROWS:(n + 1) * ROWS],
                                                vT0[rows, h // 2, u * KEYS:(u + 1) * KEYS], wo0_sb[rows, h // 2, :],
                                                start=True, stop=True)
                last.then_inc(vw_ps[0], 1)

            def up0(g):
                u, c = divmod(g, CH0)
                if c == 0:
                    pe.wait_ge(xt_lo, UNITS + u + 1)
                if g == 0:
                    pe.wait_ge(raw_split, 1)
                    pe.wait_ge(s_sb[0], TILES)
                if g == 2:
                    pe.wait_ge(pt_sb[0], TILES - 1)
                if g >= 3:
                    pe.wait_ge(h0_lo, g - 2)
                w = slice(c * ROWS, (c + 1) * ROWS)
                product(HBANK[g % 3][:], (ff0h[:, w], ff0l[:, w]), (xth[:, xt(u)], xtl[:, xt(u)])).then_inc(h0_ps, 1)

            def down0(g):
                u, c = divmod(g, CH0)
                pe.wait_ge(h0_lo, g + 1)
                if c == 0:
                    if u >= 1:
                        pe.wait_ge(o1_sb, u)
                    else:
                        pe.wait_ge(x_new[0], UNITS)
                w = slice(DFF0 + c * D, DFF0 + (c + 1) * D)
                nc.tensor.matmul(OT[:], ff0h[:, w], acth[:, g % 3, :], start=(c == 0), stop=False)
                nc.tensor.matmul(OT[:], ff0h[:, w], actl[:, g % 3, :], start=False, stop=False)
                return nc.tensor.matmul(OT[:], ff0l[:, w], acth[:, g % 3, :], start=False, stop=(c == CH0 - 1))

            def gate_logits(u):
                if u >= 1:
                    pe.wait_ge(gate_sb, u)
                w = slice(DFF0 + CH0 * D, DFF0 + CH0 * D + EXPERTS)
                for k in range(PER_UNIT):
                    tok = slice(u * UTOK + k * ROWS, u * UTOK + (k + 1) * ROWS)
                    last = product(AUX[:, k * EXPERTS:(k + 1) * EXPERTS], (xth[:, tok], xtl[:, tok]),
                                   (ff0h[:, w], ff0l[:, w]))
                last.then_inc(gate_ps, 1)

            def make_g1(u):
                pe.wait_ge(kvb_done, 2 * u + 1)
                if u >= 1:
                    pe.wait_ge(vw_sb[1], u)
                nc.tensor.matmul(BANK[5][:], wq1_sb, KB[:, u, :], start=True, stop=True).then_inc(g_ps[1], 1)

            def make_vw1(u):
                pe.wait_ge(kvb_done, 2 * u + 2)
                pe.wait_ge(g_lo[1], u + 1)
                for c in range(4):
                    last = nc.tensor.matmul(BANK[5][:, c * ROWS:(c + 1) * ROWS], VB[:, u, c * ROWS:(c + 1) * ROWS],
                                            wo1_sb, start=True, stop=True)
                last.then_inc(vw_ps[1], 1)

            def begin_ffn(s):
                if s in (1, 2):
                    make_vw0(s - 1)
                if s >= TILES + LAG_AV - 3:
                    up0(s - (TILES + LAG_AV - 3))

            pe.wait_ge(g_lo[0], 2)
            pe.wait_ge(kv1_done, 1)
            pe.wait_ge(consts, 4)
            attention(0, begin_ffn)

            for g in range(UNITS * CH0):
                u, c = divmod(g, CH0)
                if c == 0:
                    transpose_x(UNITS + u + 1)
                    gate_logits(u)
                    if u >= 1:
                        transpose_back(u - 1)
                last = down0(g)
                if g + 3 < UNITS * CH0:
                    up0(g + 3)
                if c == 1:
                    make_g1(u)
                if c == 3:
                    last.then_inc(o_ps[1], 1)
                    if u < UNITS - 1:
                        make_vw1(u)

            def up(u, j):
                c = j % NG
                tok = bass.ds((u + j // NG) * UTOK, UTOK)
                xs = (xth[:, tok], xtl[:, tok])
                if isinstance(u, int) and u == 0 and j == 0:
                    pe.wait_ge(raw_split, 1 + LOADS)
                    pe.wait_ge(xt_lo, 3 * UNITS + 1)
                    pe.wait_ge(s_sb[1], TILES)
                if isinstance(u, int) and u == 0 and j == 1:
                    pe.wait_ge(pt_sb[1], TILES)
                if j == NG:
                    pe.wait_ge(xt_lo, u + (3 * UNITS + 2))
                if not (isinstance(u, int) and u == 0 and j < 2):
                    pe.wait_ge(act_done, u * NG + (j - 1))
                for k, (bank, done) in enumerate(((hbank(j), h_ps), (vbank(j), v_ps))):
                    w = slice(k * ROWS, (k + 1) * ROWS)
                    product(bank[:], (ewh[:, c, w], ewl[:, c, w]), xs).then_inc(done, 1)

            def down(u, j):
                c, r = j % NG, j % 3
                pe.wait_ge(act_lo, u * NG + (j + 1))
                if j == P_GL and not isinstance(u, int):
                    pe.wait_ge(glT_sb, u + 2)
                if j == NG:
                    pe.wait_ge(sum_sb, u + 1)
                elif c == 0:
                    pe.wait_ge(x_new[2], UNITS)
                w = slice(2 * ROWS, 3 * ROWS)
                nc.tensor.matmul(OT[:], ewh[:, c, w], acth[:, r, :], start=(c == 0), stop=False)
                nc.tensor.matmul(OT[:], ewh[:, c, w], actl[:, r, :], start=False, stop=False)
                last = nc.tensor.matmul(OT[:], ewl[:, c, w], acth[:, r, :], start=False, stop=(c == NG - 1))
                if c == NG - 1:
                    last.then_inc(o_ps[3], 1)
                elif isinstance(u, int) and u == UNITS - 1 and j == NG - 4:
                    last.then_inc(last_slot, 1)

            def experts(u, j0, j1, last_up):
                for j in range(j0, j1):
                    if j + AHEAD <= last_up:
                        up(u, j + AHEAD)
                    if j == NG + BACK_AT:
                        back(u)
                    down(u, j)
                    if not isinstance(u, int):
                        prepare(u + 1, j)

            def back(u):
                pe.wait_ge(sum_sb, u + 1)
                pe.wait_ge(x_new[2], UNITS)
                for k in range(PER_UNIT):
                    last = nc.tensor.transpose(OB[:, k * ROWS:(k + 1) * ROWS], acc[:, k * ROWS:(k + 1) * ROWS], ident)
                last.then_inc(b_ps[3], 1)

            def gate_logits_t(n):
                w = slice(DFF0 + CH0 * D + EXPERTS, FF0COLS)
                xs = bass.ds(n * UTOK, UTOK)
                pe.wait_ge(xt_lo, n + (3 * UNITS + 1))
                product(AUX[:], (ff0h[:, w], ff0l[:, w]), (xth[:, xs], xtl[:, xs])).then_inc(glT_ps, 1)

            def gate_logits_back(n):
                for k in range(PER_UNIT):
                    last = nc.tensor.transpose(XT[:, k * EXPERTS:(k + 1) * EXPERTS],
                                               glT[:, k * ROWS:(k + 1) * ROWS], square_sb[0:EXPERTS, 0:EXPERTS])
                last.then_inc(gl_ps, 1)

            def gate_weights_t(n):
                pe.wait_ge(w1_done, n + 1)
                for k in range(PER_UNIT):
                    last = nc.tensor.transpose(AUX[0:EXPERTS, k * ROWS:(k + 1) * ROWS], gw[:, k, :], ident)
                last.then_inc(wT_ps, 1)

            def prepare(n, j):
                if j == P_XT:
                    pe.wait_ge(xn_done, n + (3 * UNITS + 1))
                    for k in range(PER_UNIT):
                        last = nc.tensor.transpose(XT[:, k * ROWS:(k + 1) * ROWS], xn[:, 0, k, :], ident)
                    last.then_inc(xt_ps, 1)
                if j == P_GLT:
                    gate_logits_t(n)
                if j == P_GL:
                    gate_logits_back(n)
                if j == P_WT:
                    gate_weights_t(n)

            def begin_experts(s):
                if s == 1:
                    make_vw1(UNITS - 1)
                    transpose_back(UNITS - 1)
                if s == TAIL_GLT:
                    gate_logits_t(0)
                if s == TAIL_GL:
                    pe.wait_ge(glT_sb, 1)
                    gate_logits_back(0)
                if s == TILES + LAG_AV - 3:
                    up(0, 0)
                if s == TAIL_WT:
                    gate_weights_t(0)
                if s == TILES + LAG_AV - 1:
                    up(0, 1)

            pe.wait_ge(mask_done, 1)
            attention(1, begin_experts)
            up(0, 2)
            experts(0, 0, EDGE, EDGE - 1 + AHEAD)
            with pe.Fori(0, UNITS - 1) as u:
                experts(u, EDGE, NG + EDGE, NG + EDGE - 1 + AHEAD)
            experts(UNITS - 1, EDGE, NG, NG - 1)
            back(UNITS - 1)


def kernel(**inputs):
    import numpy as np
    import concourse.bacc as bacc
    from concourse.bass_utils import run_bass_kernel_spmd

    a = {k: np.asarray(v) for k, v in inputs.items()}

    def rows(w, n):
        out = np.zeros((n * ROWS, w.shape[1]), w.dtype)
        out[:w.shape[0]] = w
        return out.reshape(n, ROWS, w.shape[1]).transpose(1, 0, 2).reshape(ROWS, -1)

    chunks = [[(e, ROWS * k + r) for r in range(ROWS)] for e in range(1 + EXPERTS) for k in range(FULL)]
    first = FULL * ROWS
    for p in range(PACKED):
        chunks.append([(e, first + p * PACK + r) for e in range(1, 1 + EXPERTS) for r in range(PACK)])
    ends = [(e, first + PACKED * PACK + r) for e in range(1, 1 + EXPERTS) for r in range(ENDS)]
    ends += [(0, first + r) for r in range(REST)]
    chunks.append(ends + [(0, HID)] * (ROWS - len(ends)))
    idx = np.array(chunks)

    def hidden_rows(shared, routed):
        w = np.concatenate([shared[None], routed])
        w = np.concatenate([w, np.zeros((1 + EXPERTS, 1, D), w.dtype)], axis=1)
        return w[idx[..., 0], idx[..., 1]]

    w1 = hidden_rows(a["L1_ffn_Ws1"], a["L1_ffn_W1"]).transpose(0, 2, 1)
    w2 = hidden_rows(a["L1_ffn_Ws2"], a["L1_ffn_W2"]).transpose(0, 2, 1)
    w3 = hidden_rows(a["L1_ffn_Ws3"].T, a["L1_ffn_W3"].transpose(0, 2, 1))
    ew = np.stack([w1, w2, w3], axis=2)
    ew = ew.reshape(LOADS, PER_LOAD, ROWS, CCOLS).transpose(0, 2, 1, 3).reshape(LOADS, ROWS, PER_LOAD * CCOLS)
    arrays = {
        "x": a["x"].reshape(UNITS, PER_UNIT, ROWS, D).transpose(0, 2, 1, 3),
        "ctx_wk0": np.concatenate([a["ctx_768"].reshape(UNITS * KEYS, CTX).T, a["L0_xattn_Wk"]], axis=1),
        "wv0": a["L0_xattn_Wv"],
        "wq0t": a["L0_xattn_Wq"].reshape(D, 4, 2, 64).transpose(2, 3, 1, 0).reshape(ROWS, 4, D),
        "wo0": a["L0_xattn_Wout"].reshape(4, 2, 64, D).transpose(1, 2, 0, 3).reshape(ROWS, 4, D),
        "wkv1": np.stack([a["L1_xattn_Wk"], a["L1_xattn_Wv"]], axis=1),
        "square_w": np.concatenate([np.eye(ROWS, dtype=np.float32), a["L1_xattn_Wq"].T, a["L1_xattn_Wo"],
                                    np.repeat(np.eye(HEADS[1], dtype=np.float32), HEAD_DIM[1], axis=0)], axis=1),
        "small": np.concatenate([a["g_xattn"], a["g_ffn"], a["L1_ffn_routing_bias"]]).reshape(1, -1),
        "bout": a["L0_xattn_bout"].reshape(1, D),
        "mask": a["mask_BxS2_bf1"].view(np.uint8).reshape(1, -1),
        "ff0": np.concatenate([a["L0_ffn_w1"], rows(a["L0_ffn_w2"], CH0), a["L0_ffn_Wg"], a["L1_ffn_Wg"].T,
                               np.zeros((D, ROWS - EXPERTS), np.float32)], axis=1),
        "ew": ew,
    }
    arrays = {k: np.ascontiguousarray(v) for k, v in arrays.items()}
    nc = bacc.Bacc("TRN2", target_bir_lowering=False, num_devices=1)
    args = {k: nc.dram_tensor(k + "_dram", v.shape, mybir.dt.from_np(v.dtype), kind="ExternalInput").ap()
            for k, v in arrays.items()}
    scratch = nc.dram_tensor("gate_scratch", (UNITS * EXPERTS, UTOK), mybir.dt.float32, kind="Internal").ap()
    out = nc.dram_tensor("out_dram", (UNITS, ROWS, PER_UNIT, D), mybir.dt.float32, kind="ExternalOutput").ap()
    flamingo_kernel(nc, **args, gate_scratch=scratch, out=out)
    r = run_bass_kernel_spmd(nc, [{k + "_dram": v for k, v in arrays.items()}], core_ids=[0])
    got = np.asarray(r.results[0]["out_dram"])
    return np.ascontiguousarray(got.transpose(0, 2, 1, 3)).reshape(UNITS, UTOK, D)
```
